# Optimizing a Trainium2 kernel written in Bass

```python
import numpy as np
import jax
import jax.numpy as jnp

def _softmax(x, axis=-1):
    return jax.nn.softmax(x, axis=axis)

def _gelu(x):
    return jax.nn.gelu(x, approximate=True)

def _silu(x):
    return jax.nn.silu(x)

def _sigmoid(x):
    return jax.nn.sigmoid(x)

def _layernorm(x, axis=-1, eps=1e-05):
    m = jnp.mean(x, axis=axis, keepdims=True)
    v = jnp.var(x, axis=axis, keepdims=True)
    return (x - m) / jnp.sqrt(v + eps)

def _scatter_add(tgt, idx, src, axis=0):
    return tgt.at[idx].add(src)

def _segment_sum(src, seg, n):
    return jax.ops.segment_sum(src, seg, n)
kernel_name = 'mk_decoder_preln_d1_seqx_r2_945b1c'

def setup_inputs(seed: int=0):
    np.random.seed(seed)
    _w = jnp.asarray

    def _rec_inputs():
        import jax
        import jax.numpy as jnp
        _rk = jax.random.key(seed)
        x = -0.0002928 + 1 * jax.random.normal(jax.random.fold_in(_rk, 1), (4, 1024, 512), jnp.float32)
        _lenS = 1024 - jax.random.randint(jax.random.fold_in(_rk, 7), (4,), 0, max(1, 1024 // 4) + 1, jnp.int32)
        _lenS2 = 64 - jax.random.randint(jax.random.fold_in(_rk, 8), (4,), 0, max(1, 64 // 4) + 1, jnp.int32)
        _ctx_1024P = jax.random.normal(jax.random.fold_in(_rk, 11), (4, 16, 512), jnp.float32)
        _ctx_1024c = jax.random.dirichlet(jax.random.fold_in(_rk, 511), 0.3 * jnp.ones((16,), jnp.float32), (4, 64))
        _ctx_1024t = jnp.einsum('bsk,bkd->bsd', _ctx_1024c, _ctx_1024P)
        _ctx_1024t = _ctx_1024t * jax.lax.rsqrt(jnp.mean(jnp.square(_ctx_1024t)) + 1e-12) * 0.953939
        ctx_1024 = -1.39393e-06 + 0.999914 * (_ctx_1024t + 0.3 * jax.random.normal(jax.random.fold_in(_rk, 611), (4, 64, 512), jnp.float32))
        _validS = jnp.arange(1024)[None, :] < _lenS[:, None]
        _validS2 = jnp.arange(64)[None, :] < _lenS2[:, None]
        _causal = jnp.tril(jnp.ones((1024, 1024), dtype=bool))
        mask_Bx1xSxS2_ik1 = jnp.where(jnp.broadcast_to(_validS2[:, None, None, :], (4, 1, 1024, 64)), 1, 0).astype(jnp.int32)
        return (x, ctx_1024, mask_Bx1xSxS2_ik1)
    x, ctx_1024, mask_Bx1xSxS2_ik1 = _rec_inputs()

    def _L0_attn_setup():
        import jax, jax.numpy as jnp
        import numpy as np
        B, S, E, H, BS = (4, 2048, 512, 512, 128)
        key = jax.random.key(seed)
        k1, k2, k3, k4 = jax.random.split(key, 4)
        x = jax.random.normal(k1, (B, S, E), dtype=jnp.float32)
        W_qkv = jax.random.normal(k2, (E, 3 * H), dtype=jnp.float32) * E ** (-0.5)
        W_out = jax.random.normal(k3, (H, H), dtype=jnp.float32) * H ** (-0.5)
        b_out = jax.random.normal(k4, (H,), dtype=jnp.float32) * 0.01
        return {'x': x, 'W_qkv': W_qkv, 'W_out': W_out, 'b_out': b_out}
    _L0_attn_all = _L0_attn_setup()
    _L0_attn_in = {k: v for k, v in _L0_attn_all.items() if k in ('W_qkv', 'W_out', 'b_out')}
    del _L0_attn_all

    def _L0_xattn_setup():
        import jax, jax.numpy as jnp
        import numpy as np
        HIDDEN = 512
        HEADS = 16
        HEAD_DIM = HIDDEN // HEADS
        SCALE = HEAD_DIM ** (-0.5)
        NEG_INF = -1000000000.0

        def _split_heads(x):
            B, S, _ = x.shape
            return x.reshape(B, S, HEADS, HEAD_DIM).transpose(0, 2, 1, 3)
        key = jax.random.key(seed)
        ks = jax.random.split(key, 12)
        B, Sq, Sk = (2, 1024, 1024)
        inp = {'query': jax.random.normal(ks[0], (B, Sq, HIDDEN), jnp.float32), 'key': jax.random.normal(ks[1], (B, Sk, HIDDEN), jnp.float32), 'value': jax.random.normal(ks[2], (B, Sk, HIDDEN), jnp.float32), 'mask': jax.random.randint(ks[3], (B, 1, Sq, Sk), 0, 2, jnp.int32), 'Wq': jax.random.normal(ks[4], (HIDDEN, HIDDEN), jnp.float32) * 0.02, 'bq': jax.random.normal(ks[5], (HIDDEN,), jnp.float32) * 0.02, 'Wk': jax.random.normal(ks[6], (HIDDEN, HIDDEN), jnp.float32) * 0.02, 'bk': jax.random.normal(ks[7], (HIDDEN,), jnp.float32) * 0.02, 'Wv': jax.random.normal(ks[8], (HIDDEN, HIDDEN), jnp.float32) * 0.02, 'bv': jax.random.normal(ks[9], (HIDDEN,), jnp.float32) * 0.02, 'Wo': jax.random.normal(ks[10], (HIDDEN, HIDDEN), jnp.float32) * 0.02}
        return inp
    _L0_xattn_all = _L0_xattn_setup()
    _L0_xattn_in = {k: v for k, v in _L0_xattn_all.items() if k in ('Wq', 'bq', 'Wk', 'bk', 'Wv', 'bv', 'Wo')}
    del _L0_xattn_all

    def _L0_ffn_setup():
        import jax, jax.numpy as jnp
        import numpy as np
        N_EMBD = 512
        N_STATE = 2048
        key = jax.random.key(seed)
        k_x, k_w1, k_b1, k_w2, k_b2 = jax.random.split(key, 5)
        x = jax.random.normal(k_x, (4, 1024, N_EMBD), dtype=jnp.float32)
        w1 = jax.random.normal(k_w1, (N_EMBD, N_STATE), dtype=jnp.float32) * (1.0 / np.sqrt(N_EMBD))
        b1 = jax.random.normal(k_b1, (N_STATE,), dtype=jnp.float32) * 0.02
        w2 = jax.random.normal(k_w2, (N_STATE, N_EMBD), dtype=jnp.float32) * (1.0 / np.sqrt(N_STATE))
        b2 = jax.random.normal(k_b2, (N_EMBD,), dtype=jnp.float32) * 0.02
        return {'x': x, 'w1': w1, 'b1': b1, 'w2': w2, 'b2': b2}
    _L0_ffn_all = _L0_ffn_setup()
    _L0_ffn_in = {k: v for k, v in _L0_ffn_all.items() if k in ('w1', 'b1', 'w2', 'b2')}
    del _L0_ffn_all
    return {'x': x, 'ctx_1024': ctx_1024, 'mask_Bx1xSxS2_ik1': mask_Bx1xSxS2_ik1, 'L0_attn_W_qkv': _L0_attn_in['W_qkv'], 'L0_attn_W_out': _L0_attn_in['W_out'], 'L0_attn_b_out': _L0_attn_in['b_out'], 'L0_xattn_Wq': _L0_xattn_in['Wq'], 'L0_xattn_bq': _L0_xattn_in['bq'], 'L0_xattn_Wk': _L0_xattn_in['Wk'], 'L0_xattn_bk': _L0_xattn_in['bk'], 'L0_xattn_Wv': _L0_xattn_in['Wv'], 'L0_xattn_bv': _L0_xattn_in['bv'], 'L0_xattn_Wo': _L0_xattn_in['Wo'], 'L0_ffn_w1': _L0_ffn_in['w1'], 'L0_ffn_b1': _L0_ffn_in['b1'], 'L0_ffn_w2': _L0_ffn_in['w2'], 'L0_ffn_b2': _L0_ffn_in['b2']}

def reference(x, ctx_1024, mask_Bx1xSxS2_ik1, L0_attn_W_qkv, L0_attn_W_out, L0_attn_b_out, L0_xattn_Wq, L0_xattn_bq, L0_xattn_Wk, L0_xattn_bk, L0_xattn_Wv, L0_xattn_bv, L0_xattn_Wo, L0_ffn_w1, L0_ffn_b1, L0_ffn_w2, L0_ffn_b2):
    import jax
    import jax.numpy as jnp

    def _L0_attn_ref(x, W_qkv, W_out, b_out):
        import jax, jax.numpy as jnp
        import numpy as np
        B, S, E, H, BS = (4, 2048, 512, 512, 128)
        b, s, e = x.shape
        h = W_out.shape[1]
        nb = s // BS
        qkv = x @ W_qkv
        q, k, v = jnp.split(qkv, 3, axis=-1)

        def blk(t):
            return t.reshape(b, nb, BS, h)
        scale = h ** (-0.5)
        scores = jnp.einsum('bnqd,bnkd->bnqk', blk(q), blk(k)) * scale
        causal = jnp.tril(jnp.ones((BS, BS), dtype=bool))
        scores = jnp.where(causal, scores, -jnp.inf)
        scores = scores - jnp.max(scores, axis=-1, keepdims=True)
        p = jnp.exp(scores)
        p = p / (jnp.sum(p, axis=-1, keepdims=True) + 1e-06)
        out = jnp.einsum('bnqk,bnkd->bnqd', p, blk(v)).reshape(b, s, h)
        return out @ W_out.T + b_out

    def _L0_xattn_ref(query, key, value, mask, Wq, bq, Wk, bk, Wv, bv, Wo):
        import jax, jax.numpy as jnp
        import numpy as np
        HIDDEN = 512
        HEADS = 16
        HEAD_DIM = HIDDEN // HEADS
        SCALE = HEAD_DIM ** (-0.5)
        NEG_INF = -1000000000.0

        def _split_heads(x):
            B, S, _ = x.shape
            return x.reshape(B, S, HEADS, HEAD_DIM).transpose(0, 2, 1, 3)
        B, Sq, _ = query.shape
        q = _split_heads(query @ Wq.T + bq)
        k = _split_heads(key @ Wk.T + bk)
        v = _split_heads(value @ Wv.T + bv)
        scores = jnp.einsum('bhqd,bhkd->bhqk', q, k) * SCALE
        scores = jnp.where(mask == 0, NEG_INF, scores)
        attn = jax.nn.silu(scores)
        out = jnp.einsum('bhqk,bhkd->bhqd', attn, v)
        out = out.transpose(0, 2, 1, 3).reshape(B, Sq, HIDDEN)
        return out @ Wo.T

    def _L0_ffn_ref(x, w1, b1, w2, b2):
        import jax, jax.numpy as jnp
        import numpy as np
        N_EMBD = 512
        N_STATE = 2048
        h = jax.nn.gelu(jnp.einsum('bse,eh->bsh', x, w1) + b1, approximate=False)
        return jnp.einsum('bsh,he->bse', h, w2) + b2
    x = x + _L0_attn_ref(_layernorm(x, axis=-1), L0_attn_W_qkv, L0_attn_W_out, L0_attn_b_out)
    x = x + _L0_xattn_ref(_layernorm(x, axis=-1), ctx_1024, ctx_1024, mask_Bx1xSxS2_ik1, L0_xattn_Wq, L0_xattn_bq, L0_xattn_Wk, L0_xattn_bk, L0_xattn_Wv, L0_xattn_bv, L0_xattn_Wo)
    x = x + _L0_ffn_ref(_layernorm(x, axis=-1), L0_ffn_w1, L0_ffn_b1, L0_ffn_w2, L0_ffn_b2)
    return x

_drawn_inputs = setup_inputs


def setup_inputs(seed=0):
    import zlib

    import numpy as np

    out = dict(_drawn_inputs(seed))
    spreads = {}
    factors = {'L0_attn_b_out': 6.182, 'L0_xattn_bq': 3.485, 'L0_ffn_b1': 5.32, 'L0_ffn_b2': 3.717}
    for name, (base, spread) in spreads.items():
        noise = np.random.default_rng([zlib.crc32(name.encode()), seed]).standard_normal(out[name].shape)
        drawn = base * np.exp(spread * noise) if base else spread * noise
        out[name] = jnp.asarray(drawn.astype(out[name].dtype))
    for name, factor in factors.items():
        out[name] = (out[name] * factor).astype(out[name].dtype)
    return out
```

```python
import concourse.bass as bass
from concourse import mybir
from contextlib import ExitStack

P = 128
BATCH, SEQ, E = 4, 1024, 512
EC = E // P
TILE = 512
NB = TILE // P
TILES = BATCH * SEQ // TILE
TILES_PER_BATCH = SEQ // TILE
KEYS = 64
HEADS, HEAD_DIM = 16, 32
PAIRS = HEADS // 2
HEADS_PER_CHUNK = P // HEAD_DIM
FF = 2048
FC = FF // P
LN_EPS = 1e-5
DEN_EPS = 1e-6
SELF_SCALE = float(E) ** -0.5
CROSS_SCALE = float(HEAD_DIM) ** -0.5
MASKED = -3.0e38
BLOCK_BANK = (7, 3, 0, 4)
PROJ_BANK = (5, 2, 6, 1)
LN3_BANK = (7, 5, 6, 4)


def decoder_layer_program(nc, x, ctxT, mask, wqkvT, woutT, b_out, xwqT, bq, xwkT, bk, xwvT, bv, xwoT,
                          w1, b1, w2, b2, out):
    fp32, fp32r, i32 = mybir.dt.float32, mybir.dt.float32r, mybir.dt.int32
    ALU, ACT, AX = mybir.AluOpType, mybir.ActivationFunctionType, mybir.AxisListType

    def product(pe, out_ap, lhs, rhs, start, stop):
        pe.matmul(out_ap, lhs[1], rhs[0], start=start, stop=False)
        pe.matmul(out_ap, lhs[0], rhs[1], start=False, stop=False)
        return pe.matmul(out_ap, lhs[0], rhs[0], start=False, stop=stop)

    def f(ap):
        return ap.bitcast(fp32)

    def cols(n, width=P):
        return slice(n * width, (n + 1) * width)

    x_blocks = x.rearrange("b (n p) e -> (b n) p e", p=P)
    out_blocks = out.rearrange("b (n p) e -> (b n) p e", p=P)
    x2_dram = nc.dram_tensor("x2_dram", (TILES * NB, P, E), fp32).ap()

    whole = ExitStack()
    with whole:
        def names(stack):
            def sb(name, shape, dt=fp32):
                return stack.enter_context(nc.sbuf_tensor(name, shape, dt))

            def pair(name, shape):
                return sb(name + "_hi", shape, fp32r), sb(name + "_lo", shape, fp32r)

            def sem(name):
                return stack.enter_context(nc.semaphore(name))
            return sb, pair, sem

        def at(hl, *index):
            return tuple(part[(slice(None),) + index] for part in hl)

        sb, pair, sem = names(whole)
        bank = [whole.enter_context(nc.psum_tensor(f"bank{i}", [P, TILE], fp32)) for i in range(8)]
        ident = sb("ident", [P, P])

        layer = ExitStack()
        with layer:
            sb, pair, sem = names(layer)
            wqk = pair("wqk", [P, EC, E])
            wvo = pair("wvo", [P, EC, E])
            wq = pair("wq", [P, EC, E])
            wo = pair("wo", [P, EC, E])
            keysT = sb("keysT", [P, EC, BATCH, KEYS])
            values = sb("values", [P, BATCH, E])
            bq_col = sb("bq_col", [P, EC])
            bout_row = sb("bout_row", [P, E])
            causal = sb("causal", [P, P])
            kb = pair("kb", [P, EC, P])
            vb = pair("vb", [P, PAIRS, P])

            setup = ExitStack()
            with setup:
                sb, pair, sem = names(setup)
                RAWS, PARTS = 3, 4
                raw = [sb(f"raw{i}", [P, EC, E]) for i in range(RAWS)]
                part = [pair(f"part{i}", [P, EC, E]) for i in range(PARTS)]
                ctx_raw = sb("ctx_raw", [P, EC, BATCH, KEYS])
                ctx2 = pair("ctx2", [P, EC, BATCH, 2, KEYS])
                bk_col = sb("bk_col", [P, EC])
                bv_row = sb("bv_row", [P, E])

                weight_loaded = [sem(f"weight_loaded{i}") for i in range(RAWS)]
                ctx_loaded, bias_loaded = sem("ctx_loaded"), sem("bias_loaded")
                weight_hi, weight_lo, weight_lo_pool = sem("weight_hi"), sem("weight_lo"), sem("weight_lo_pool")
                ctx_hi, ctx_lo = sem("ctx_hi"), sem("ctx_lo")
                filled, shaped = sem("filled"), sem("shaped")
                wqk_done, wvo_done, keys_done, values_done = (
                    sem("wqk_done"), sem("wvo_done"), sem("keys_done"), sem("values_done"))
                wqk_hi, wqk_lo, wvo_hi, wvo_lo = sem("wqk_hi"), sem("wqk_lo"), sem("wvo_hi"), sem("wvo_lo")
                keys_out, values_out = sem("keys_out"), sem("values_out")

                def rows(w):
                    return w.rearrange("(c p) n -> p c n", p=P)

                WEIGHTS = [rows(wqkvT[0:E, :]), rows(wqkvT[E:2 * E, :]), rows(wqkvT[2 * E:3 * E, :]),
                           rows(woutT), rows(xwkT), rows(xwvT), rows(xwqT), rows(xwoT)]
                TARGET = part + [part[0], part[1], wq, wo]
                ON_DVE = 4

                with nc.Block() as block:
                    @block.sync
                    def _(sp):
                        for i, w in enumerate(WEIGHTS):
                            if i >= RAWS + ON_DVE:
                                sp.wait_ge(weight_lo_pool, i - RAWS - ON_DVE + 1)
                            elif i >= RAWS:
                                sp.wait_ge(weight_lo, i - RAWS + 1)
                            sp.dma_start(raw[i % RAWS][:, :, :], w).then_inc(weight_loaded[i % RAWS], 16)
                            if i == 1:
                                sp.dma_start(ctx_raw[:, :, :, :], ctxT.rearrange("(c p) b k -> p c b k", p=P)
                                             ).then_inc(ctx_loaded, 16)
                                sp.dma_start(bk_col[:, :], bk).then_inc(bias_loaded, 16)
                                sp.dma_start(bq_col[:, :], bq).then_inc(bias_loaded, 16)
                                sp.dma_start(bv_row[:, :], bv.partition_broadcast(P)).then_inc(bias_loaded, 16)
                                sp.dma_start(bout_row[:, :], b_out.partition_broadcast(P)).then_inc(bias_loaded, 16)

                    @block.scalar
                    def _(act):
                        def split_hi(i):
                            act.wait_ge(weight_loaded[i % RAWS], 16 * (i // RAWS + 1))
                            if i == 4:
                                act.wait_ge(wqk_done, EC)
                            act.activation(TARGET[i][0][:, :, :], raw[i % RAWS][:, :, :], ACT.Copy
                                           ).then_inc(weight_hi, 1)

                        def evacuate_hi(hl, banks, done, made):
                            for m in range(EC):
                                act.wait_ge(done, m + 1)
                                act.activation(hl[0][:, m, :], bank[banks + m][:, :], ACT.Copy).then_inc(made, 1)

                        for i in range(4):
                            split_hi(i)
                        act.wait_ge(ctx_loaded, 16)
                        for d in range(2):
                            act.activation(ctx2[0][:, :, :, d, :], ctx_raw[:, :, :, :], ACT.Copy
                                           ).then_inc(ctx_hi, 1)
                        evacuate_hi(wqk, 0, wqk_done, wqk_hi)
                        split_hi(4)
                        split_hi(5)
                        evacuate_hi(wvo, 4, wvo_done, wvo_hi)
                        split_hi(6)
                        split_hi(7)
                        act.wait_ge(bias_loaded, 64)
                        for m in range(EC):
                            act.wait_ge(keys_done, m + 1)
                            act.activation(keysT[:, m, :, :], bank[m][:, 0:BATCH * KEYS].rearrange(
                                "p (b k) -> p b k", b=BATCH), ACT.Identity, bias=bk_col[:, m:m + 1]
                                ).then_inc(keys_out, 1)

                    @block.vector
                    def _(dve):
                        def evacuate_lo(hl, banks, hi, made):
                            for m in range(EC):
                                dve.wait_ge(hi, m + 1)
                                dve.tensor_tensor(hl[1][:, m, :], bank[banks + m][:, :], f(hl[0][:, m, :]),
                                                  ALU.subtract).then_inc(made, 1)

                        for i in range(ON_DVE):
                            dve.wait_ge(weight_hi, i + 1)
                            dve.tensor_tensor(TARGET[i][1][:, :, :], raw[i % RAWS][:, :, :], f(TARGET[i][0][:, :, :]),
                                              ALU.subtract).then_inc(weight_lo, 1)
                        for d in range(2):
                            dve.wait_ge(ctx_hi, d + 1)
                            dve.tensor_tensor(ctx2[1][:, :, :, d, :], ctx_raw[:, :, :, :],
                                              f(ctx2[0][:, :, :, d, :]), ALU.subtract).then_inc(ctx_lo, 1)
                        evacuate_lo(wqk, 0, wqk_hi, wqk_lo)
                        evacuate_lo(wvo, 4, wvo_hi, wvo_lo)
                        dve.wait_ge(bias_loaded, 64)
                        for b in range(BATCH):
                            dve.wait_ge(values_done, b + 1)
                            dve.tensor_tensor(values[:, b, :], bank[4 + b][:, :], bv_row[:, :], ALU.add
                                              ).then_inc(values_out, 1)

                    @block.gpsimd
                    def _(pool):
                        pool.memset(ident[:, :], 0.0).then_inc(filled, 1)
                        pool.memset(causal[:, :], 0.0).then_inc(filled, 1)
                        for part_ in (*kb, *vb):
                            pool.memset(f(part_[:, :, :]), 0.0).then_inc(filled, 1)
                        pool.wait_ge(filled, 6)
                        pool.affine_select(out=ident[:, :], in_=ident[:, :], compare_op=ALU.not_equal, fill=1.0,
                                           base=0, pattern=[[-1, P]], channel_multiplier=1).then_inc(shaped, 1)
                        pool.affine_select(out=causal[:, :], in_=causal[:, :], compare_op=ALU.is_ge, fill=MASKED,
                                           base=0, pattern=[[-1, P]], channel_multiplier=1).then_inc(shaped, 1)
                        for i in range(ON_DVE, 8):
                            pool.wait_ge(weight_hi, i + 1)
                            pool.tensor_tensor(TARGET[i][1][:, :, :], raw[i % RAWS][:, :, :],
                                               f(TARGET[i][0][:, :, :]), ALU.subtract).then_inc(weight_lo_pool, 1)
                        pool.wait_ge(shaped, 2)

                    @block.tensor
                    def _(pe):
                        def fold(lhs, rhs, banks, done):
                            for m in range(EC):
                                for c in range(EC):
                                    last = product(pe, bank[banks + m][:, :], at(lhs, c, cols(m)), at(rhs, c),
                                                   c == 0, c == EC - 1)
                                last.then_inc(done, 1)

                        pe.wait_ge(weight_lo, 2)
                        fold(part[0], part[1], 0, wqk_done)
                        pe.wait_ge(weight_lo, 4)
                        fold(part[2], part[3], 4, wvo_done)
                        pe.wait_ge(weight_lo_pool, 1)
                        pe.wait_ge(ctx_lo, 2)
                        pe.wait_ge(wqk_lo, EC)
                        for m in range(EC):
                            for c in range(EC):
                                last = product(pe, bank[m][:, 0:BATCH * KEYS], at(part[0], c, cols(m)),
                                               at(ctx2, c, slice(None), 0), c == 0, c == EC - 1)
                            last.then_inc(keys_done, 1)
                        pe.wait_ge(weight_lo_pool, 2)
                        pe.wait_ge(wvo_lo, EC)
                        for b in range(BATCH):
                            for c in range(EC):
                                last = product(pe, bank[4 + b][:, :], at(ctx2, c, b), at(part[1], c),
                                               c == 0, c == EC - 1)
                            last.then_inc(values_done, 1)

            both = ExitStack()
            with both:
                sb, pair, sem = names(both)
                x_in = sb("x_in", [P, NB, E])
                x1 = sb("x1", [P, 2, NB, E])
                zn = sb("zn", [P, NB, E])
                zT = pair("zT", [P, EC, TILE])
                yv = pair("yv", [P, EC, TILE])
                qo = pair("qo", [P, EC, TILE])
                attn = pair("attn", [P, 4, TILE])
                act_in = sb("act_in", [P, 3, TILE])
                mask_i = sb("mask_i", [P, TILE], i32)
                mask_f = sb("mask_f", [P, TILE])
                keys_now = sb("keys_now", [P, EC, KEYS])
                values_now = sb("values_now", [P, E])
                prob = sb("prob", [P, NB, P])
                probT = pair("probT", [P, TILE])
                stats = sb("stats", [P, NB, 6])
                mv1, mv2 = sb("mv1", [P, NB, 2]), sb("mv2", [P, NB, 2])
                ve1, ve2 = sb("ve1", [P, NB]), sb("ve2", [P, NB])
                rstd1, rstd2 = sb("rstd1", [P, NB]), sb("rstd2", [P, NB])
                minus_half = sb("minus_half", [P, NB])
                nmax, nbias = sb("nmax", [P, NB]), sb("nbias", [P, NB])
                sums, den, rden = sb("sums", [P, NB]), sb("den", [P, NB]), sb("rden", [P, NB])

                x_loaded = [sem(f"x_loaded{i}") for i in range(NB)]
                x2_stored = [sem(f"x2_stored{i}") for i in range(NB)]
                mask_loaded, mask_ready = sem("mask_loaded"), sem("mask_ready")
                z1T_done, y_done, s1_done, v_done, pT_done, pv_done = (
                    sem("z1T_done"), sem("y_done"), sem("s1_done"), sem("v_done"), sem("pT_done"), sem("pv_done"))
                q_done, s2_done, o_done, proj_done, z2T_done = (
                    sem("q_done"), sem("s2_done"), sem("o_done"), sem("proj_done"), sem("z2T_done"))
                z1T_hi, y_hi, v_hi, pT_hi, q_hi, o_hi, z2T_hi = (
                    sem("z1T_hi"), sem("y_hi"), sem("v_hi"), sem("pT_hi"), sem("q_hi"), sem("o_hi"), sem("z2T_hi"))
                z1T_lo, y_lo, v_lo, pT_lo, q_lo, o_lo, z2T_lo = (
                    sem("z1T_lo"), sem("y_lo"), sem("v_lo"), sem("pT_lo"), sem("q_lo"), sem("o_lo"), sem("z2T_lo"))
                s1_masked, s1_max, s1_bias, s1_exp, s1_den, s1_rden, prob_ready = (
                    sem("s1_masked"), sem("s1_max"), sem("s1_bias"), sem("s1_exp"), sem("s1_den"),
                    sem("s1_rden"), sem("prob_ready"))
                s2_masked, attn_full, attn_lo = sem("s2_masked"), sem("attn_full"), sem("attn_lo")
                kv_now, kv_hi, kv_ready = sem("kv_now"), sem("kv_hi"), sem("kv_ready")
                half_set = sem("half_set")
                ln1_stats, ln1_mv, ln1_ve, ln1_rstd, z1_ready, x_biased = (
                    sem("ln1_stats"), sem("ln1_mv"), sem("ln1_ve"), sem("ln1_rstd"), sem("z1_ready"),
                    sem("x_biased"))
                ln2_stats, ln2_mv, ln2_ve, ln2_rstd, z2_ready = (
                    sem("ln2_stats"), sem("ln2_mv"), sem("ln2_ve"), sem("ln2_rstd"), sem("z2_ready"))
                x1_ready, x2_ready = sem("x1_ready"), sem("x2_ready")

                def chunks(ap):
                    return ap.rearrange("p (c t) -> p c t", c=EC)

                BLOCKS = []
                for h in range(HEADS_PER_CHUNK):
                    r = cols(h, HEAD_DIM)
                    BLOCKS.append((tuple(k[r, :, cols(h % 2, KEYS)] for k in kb), keys_now[r, :, :]))
                for h in range(HEADS_PER_CHUNK):
                    r = cols(h % 2, KEYS)
                    BLOCKS.append((
                        tuple(v[r, :, :].rearrange("p (m o) n -> p m o n", o=2)[:, :, h // 2, cols(h, HEAD_DIM)]
                              for v in vb),
                        values_now[r, :].rearrange("p (m h e) -> p m h e", m=EC, e=HEAD_DIM)[:, :, h, :]))

                def pipeline(engine, step):
                    step(0, None, 0)
                    step(1, 0, 1)
                    with engine.Fori(0, (TILES - 2) // 2) as n:
                        for u in range(2):
                            step(2 * n + u + 2, 2 * n + u + 1, u)
                    step(None, TILES - 1, 0)

                def first(t):
                    return isinstance(t, int) and t == 0

                with nc.Block() as block:
                    @block.sync
                    def _(sp):
                        def load_mask(t):
                            for d in range(2):
                                sp.dma_start(mask_i[d * KEYS:(d + 1) * KEYS, :], mask[t, :, :]
                                             ).then_inc(mask_loaded, 16)

                        def load_x(t, i):
                            sp.dma_start(x_in[:, i, :], x_blocks[t * NB + i, :, :]).then_inc(x_loaded[i], 16)

                        for i in range(NB):
                            load_x(0, i)
                        load_mask(0)
                        with sp.Fori(0, TILES - 1) as t:
                            for i in range(NB):
                                sp.wait_ge(x1_ready, NB * t + i + 1)
                                load_x(t + 1, i)
                            sp.wait_ge(mask_ready, t + 1)
                            load_mask(t + 1)

                    @block.gpsimd
                    def _(pool):
                        def rstd(mv, mv_ready, ve, ve_ready, rs, rs_ready, t):
                            pool.wait_ge(mv_ready, NB * (t + 1))
                            pool.nop(nofuse=True)
                            pool.tensor_scalar(ve[:, :], mv[:, :, 1], LN_EPS, None, ALU.add).then_inc(ve_ready, 1)
                            pool.wait_ge(ve_ready, t + 1)
                            pool.tensor_tensor(rs[:, :], ve[:, :], minus_half[:, :], ALU.pow).then_inc(rs_ready, 1)

                        def step(a, b, par):
                            if b is not None:
                                batch = b // TILES_PER_BATCH
                                pool.tensor_copy(keys_now[:, :, :], keysT[:, :, batch, :]).then_inc(kv_now, 1)
                                pool.tensor_copy(values_now[:, :], values[:, batch, :]).then_inc(kv_now, 1)
                            if a is not None:
                                rstd(mv1, ln1_mv, ve1, ln1_ve, rstd1, ln1_rstd, a)
                                pool.wait_ge(ln1_rstd, a + 1)
                                if not first(a):
                                    pool.wait_ge(z2T_done, NB * a)
                                pool.nop(nofuse=True)
                                for i in range(NB):
                                    pool.tensor_scalar(zn[:, i, :], x_in[:, i, :], mv1[:, i, 0:1],
                                                       rstd1[:, i:i + 1], ALU.subtract, ALU.mult
                                                       ).then_inc(z1_ready, 1)
                            if b is not None:
                                for j in range(4):
                                    silu_lo(b, j)
                            if a is not None:
                                pool.wait_ge(z1_ready, NB * (a + 1))
                                for i in range(NB):
                                    pool.tensor_tensor(x_in[:, i, :], x_in[:, i, :], bout_row[:, :], ALU.add
                                                       ).then_inc(x_biased, 1)
                            if b is not None:
                                for j in range(4, 8):
                                    silu_lo(b, j)
                            if a is not None:
                                rstd(mv2, ln2_mv, ve2, ln2_ve, rstd2, ln2_rstd, a)

                        def silu_lo(b, j):
                            pool.wait_ge(attn_full, PAIRS * b + j + 1)
                            pool.tensor_tensor(attn[1][:, j % 4, :], act_in[:, j % 3, :], f(attn[0][:, j % 4, :]),
                                               ALU.subtract).then_inc(attn_lo, 1)

                        pool.memset(minus_half[:, :], -0.5).then_inc(half_set, 1)
                        pool.wait_ge(half_set, 1)
                        pipeline(pool, step)

                    @block.scalar
                    def _(act):
                        def step(a, b, par):
                            if b is not None:
                                for m in range(EC):
                                    act.wait_ge(q_done, EC * b + m + 1)
                                    act.activation(qo[0][:, m, :], bank[m][:, :], ACT.Identity,
                                                   bias=bq_col[:, m:m + 1]).then_inc(q_hi, 1)
                                act.wait_ge(kv_now, 2 * (b + 1))
                                for (hi, _), source in BLOCKS:
                                    act.activation(hi, source, ACT.Copy).then_inc(kv_hi, 1)
                            if a is not None:
                                for i in range(NB):
                                    act.wait_ge(z1T_done, NB * a + i + 1)
                                    act.activation(zT[0][:, :, cols(i)], chunks(bank[4 + i][:, :]), ACT.Copy
                                                   ).then_inc(z1T_hi, 1)
                                for m in range(EC):
                                    act.wait_ge(y_done, EC * a + m + 1)
                                    act.activation(yv[0][:, m, :], bank[m][:, :], ACT.Copy).then_inc(y_hi, 1)
                            if b is not None:
                                for j in range(4):
                                    silu(b, j)
                            if a is not None:
                                act.wait_ge(s1_bias, a + 1)
                                for i in range(NB):
                                    act.activation(prob[:, i, :], prob[:, i, :], ACT.Exp, bias=nbias[:, i:i + 1],
                                                   scale=SELF_SCALE, accum_out=sums[:, i:i + 1]
                                                   ).then_inc(s1_exp, 1)
                                v_high(a, 0, 1)
                                v_high(a, 1, 2)
                            if b is not None:
                                o_high(b, 0, 4)
                                o_high(b, 1, 5)
                                for j in range(4, 8):
                                    silu(b, j)
                            if a is not None:
                                v_high(a, 2, 4)
                                v_high(a, 3, 5)
                                act.wait_ge(pT_done, a + 1)
                                act.activation(probT[0][:, :], bank[1][:, :], ACT.Copy).then_inc(pT_hi, 1)
                            if b is not None:
                                o_high(b, 2, 2)
                                o_high(b, 3, 6)
                            if a is not None:
                                for i in range(NB):
                                    act.wait_ge(z2T_done, NB * a + i + 1)
                                    act.activation(zT[0][:, :, cols(i)], chunks(bank[BLOCK_BANK[i]][:, :]), ACT.Copy
                                                   ).then_inc(z2T_hi, 1)
                            if b is not None:
                                for i in range(NB):
                                    act.wait_ge(x2_ready, NB * b + i + 1)
                                    act.dma_start(x2_dram[b * NB + i, :, :], x1[:, 1 - par, i, :]
                                                  ).then_inc(x2_stored[i], 16)

                        def v_high(a, i, from_bank):
                            act.wait_ge(v_done, NB * a + i + 1)
                            act.activation(yv[0][:, i, :], bank[from_bank][:, :], ACT.Copy).then_inc(v_hi, 1)

                        def o_high(b, m, from_bank):
                            act.wait_ge(o_done, EC * b + m + 1)
                            act.activation(qo[0][:, m, :], bank[from_bank][:, :], ACT.Copy).then_inc(o_hi, 1)

                        def silu(b, j):
                            act.wait_ge(s2_masked, PAIRS * b + j + 1)
                            act.activation(attn[0][:, j % 4, :], act_in[:, j % 3, :], ACT.Silu)
                            act.activation(act_in[:, j % 3, :], act_in[:, j % 3, :], ACT.Silu
                                           ).then_inc(attn_full, 1)

                        pipeline(act, step)
                        for i in range(NB):
                            act.wait_ge(x2_stored[i], 16 * TILES)

                    @block.vector
                    def _(dve):
                        def row_stats(rows_of, stats_done, mv, mv_done, t):
                            for i in range(NB):
                                dve.bn_stats(stats[:, i, :], rows_of(i)).then_inc(stats_done, 1)
                            dve.wait_ge(stats_done, NB * (t + 1))
                            dve.nop(nofuse=True)
                            for i in range(NB):
                                dve.bn_aggr(mv[:, i, :], stats[:, i, :]).then_inc(mv_done, 1)

                        def low(hl, index, from_bank, hi_made, made, value):
                            dve.wait_ge(hi_made, value)
                            src = bank[from_bank][:, :]
                            hi, lo = at(hl, *index)
                            dve.tensor_tensor(lo, chunks(src) if len(index) == 2 else src, f(hi), ALU.subtract
                                              ).then_inc(made, 1)

                        def mask_scores(b, j, from_bank):
                            dve.wait_ge(s2_done, PAIRS * b + j + 1)
                            if j >= 3:
                                dve.wait_ge(attn_lo, PAIRS * b + j - 2)
                            dve.scalar_tensor_tensor(act_in[:, j % 3, :], bank[from_bank][:, :], CROSS_SCALE,
                                                     mask_f[:, :], ALU.mult, ALU.mult).then_inc(s2_masked, 1)

                        def step(a, b, par):
                            if a is not None:
                                for i in range(NB):
                                    dve.wait_ge(x_loaded[i], 16 * (a + 1))
                                dve.nop(nofuse=True)
                                row_stats(lambda i: x_in[:, i, :], ln1_stats, mv1, ln1_mv, a)
                            if b is not None:
                                dve.wait_ge(mask_loaded, 32 * (b + 1))
                                dve.tensor_scalar(mask_f[:, :], mask_i[:, :], 0.0, None, ALU.not_equal
                                                  ).then_inc(mask_ready, 1)
                                for m in range(EC):
                                    dve.wait_ge(q_hi, EC * b + m + 1)
                                    dve.scalar_tensor_tensor(qo[1][:, m, :], bank[m][:, :], bq_col[:, m:m + 1],
                                                             f(qo[0][:, m, :]), ALU.add, ALU.subtract
                                                             ).then_inc(q_lo, 1)
                                dve.wait_ge(kv_hi, len(BLOCKS) * (b + 1))
                                for (hi, lo), source in BLOCKS:
                                    dve.tensor_tensor(lo, source, f(hi), ALU.subtract).then_inc(kv_ready, 1)
                            if a is not None:
                                for i in range(NB):
                                    low(zT, (slice(None), cols(i)), 4 + i, z1T_hi, z1T_lo, NB * a + i + 1)
                                for m in range(EC):
                                    low(yv, (m,), m, y_hi, y_lo, EC * a + m + 1)
                            if b is not None:
                                dve.wait_ge(mask_ready, b + 1)
                                for j in range(4):
                                    mask_scores(b, j, 4 + j)
                            if a is not None:
                                dve.wait_ge(s1_done, a + 1)
                                for i in range(NB):
                                    dve.tensor_tensor(prob[:, i, :], bank[0][:, cols(i)], causal[:, :], ALU.add
                                                      ).then_inc(s1_masked, 1)
                                dve.wait_ge(s1_masked, NB * (a + 1))
                                dve.reduce_max(nmax[:, :], prob[:, :, :], AX.X, negate=True).then_inc(s1_max, 1)
                                dve.wait_ge(s1_max, a + 1)
                                dve.tensor_scalar(nbias[:, :], nmax[:, :], SELF_SCALE, None, ALU.mult
                                                  ).then_inc(s1_bias, 1)
                                low(yv, (0,), 1, v_hi, v_lo, NB * a + 1)
                                low(yv, (1,), 2, v_hi, v_lo, NB * a + 2)
                                dve.wait_ge(s1_exp, NB * (a + 1))
                                dve.tensor_scalar(den[:, :], sums[:, :], DEN_EPS, None, ALU.add).then_inc(s1_den, 1)
                                dve.wait_ge(s1_den, a + 1)
                                dve.reciprocal(rden[:, :], den[:, :]).then_inc(s1_rden, 1)
                                dve.wait_ge(s1_rden, a + 1)
                                for i in range(NB):
                                    dve.tensor_scalar(prob[:, i, :], prob[:, i, :], rden[:, i:i + 1], None, ALU.mult
                                                      ).then_inc(prob_ready, 1)
                            if b is not None:
                                low(qo, (0,), 4, o_hi, o_lo, EC * b + 1)
                                low(qo, (1,), 5, o_hi, o_lo, EC * b + 2)
                                for j, from_bank in zip(range(4, 8), (6, 7, 3, 0)):
                                    mask_scores(b, j, from_bank)
                            if a is not None:
                                low(yv, (2,), 4, v_hi, v_lo, NB * a + 3)
                                low(yv, (3,), 5, v_hi, v_lo, NB * a + 4)
                                dve.wait_ge(pT_hi, a + 1)
                                dve.tensor_tensor(probT[1][:, :], bank[1][:, :], f(probT[0][:, :]), ALU.subtract
                                                  ).then_inc(pT_lo, 1)
                            if b is not None:
                                low(qo, (2,), 2, o_hi, o_lo, EC * b + 3)
                                low(qo, (3,), 6, o_hi, o_lo, EC * b + 4)
                            if a is not None:
                                dve.wait_ge(x_biased, NB * (a + 1))
                                for i in range(NB):
                                    dve.wait_ge(pv_done, NB * a + i + 1)
                                    if b is not None and not first(b):
                                        dve.wait_ge(x2_stored[i], 16 * b)
                                    dve.tensor_tensor(x1[:, par, i, :], bank[BLOCK_BANK[i]][:, :], x_in[:, i, :],
                                                      ALU.add).then_inc(x1_ready, 1)
                                dve.wait_ge(x1_ready, NB * (a + 1))
                                dve.nop(nofuse=True)
                                row_stats(lambda i: x1[:, par, i, :], ln2_stats, mv2, ln2_mv, a)
                                dve.wait_ge(ln2_rstd, a + 1)
                                for i in range(NB):
                                    dve.tensor_scalar(zn[:, i, :], x1[:, par, i, :], mv2[:, i, 0:1],
                                                      rstd2[:, i:i + 1], ALU.subtract, ALU.mult
                                                      ).then_inc(z2_ready, 1)
                            if b is not None:
                                for i in range(NB):
                                    dve.wait_ge(proj_done, NB * b + i + 1)
                                    dve.tensor_tensor(x1[:, 1 - par, i, :], bank[PROJ_BANK[i]][:, :],
                                                      x1[:, 1 - par, i, :], ALU.add).then_inc(x2_ready, 1)
                            if a is not None:
                                for i in range(NB):
                                    low(zT, (slice(None), cols(i)), BLOCK_BANK[i], z2T_hi, z2T_lo, NB * a + i + 1)

                        pipeline(dve, step)

                    @block.tensor
                    def _(pe):
                        def transposed_rows(i, to_bank, done):
                            for c in range(EC):
                                last = pe.transpose(bank[to_bank][:, cols(c)], zn[:, i, cols(c)], ident[:, :])
                            last.then_inc(done, 1)

                        def project(to_bank, lhs, rhs, done):
                            for c in range(EC):
                                last = product(pe, bank[to_bank][:, :], lhs(c), rhs(c), c == 0, c == EC - 1)
                            last.then_inc(done, 1)

                        def value_rows(i, to_bank):
                            project(to_bank, lambda c: at(zT, c, cols(i)), lambda c: at(wvo, c), v_done)

                        def cross_scores(j, to_bank):
                            r = cols(j % 2, 2 * HEAD_DIM)
                            lhs = tuple(k[r, j // 2, :] for k in kb)
                            rhs = tuple(q[r, j // 2, :] for q in qo)
                            product(pe, bank[to_bank][:, :], lhs, rhs, True, True).then_inc(s2_done, 1)

                        def cross_output(b, m, to_bank):
                            pe.wait_ge(attn_lo, PAIRS * b + 2 * m + 2)
                            for n in range(2):
                                j = 2 * m + n
                                last = product(pe, bank[to_bank][:, :], at(vb, j), at(attn, j % 4), n == 0, n == 1)
                            last.then_inc(o_done, 1)

                        def step(a, b, par):
                            if b is not None:
                                pe.wait_ge(z2T_lo, NB * (b + 1))
                                for m in range(EC):
                                    if m == 1 and not first(b):
                                        pe.wait_ge(x2_ready, NB * b)
                                    project(m, lambda c: at(wq, c, cols(m)), lambda c: at(zT, c), q_done)
                            if a is not None:
                                for i in range(NB):
                                    pe.wait_ge(z1_ready, NB * a + i + 1)
                                    transposed_rows(i, 4 + i, z1T_done)
                                pe.wait_ge(z1T_lo, NB * (a + 1))
                                for m in range(EC):
                                    if b is not None:
                                        pe.wait_ge(q_lo, EC * b + m + 1)
                                    project(m, lambda c: at(wqk, c, cols(m)), lambda c: at(zT, c), y_done)
                            if b is not None:
                                pe.wait_ge(q_lo, EC * (b + 1))
                                pe.wait_ge(kv_ready, len(BLOCKS) * (b + 1))
                                for j in range(4):
                                    cross_scores(j, 4 + j)
                            if a is not None:
                                pe.wait_ge(y_lo, EC * (a + 1))
                                for i in range(NB):
                                    for c in range(EC):
                                        last = product(pe, bank[0][:, cols(i)], at(yv, c, cols(i)),
                                                       at(zT, c, cols(i)), c == 0, c == EC - 1)
                                last.then_inc(s1_done, 1)
                                value_rows(0, 1)
                                value_rows(1, 2)
                            if b is not None:
                                cross_output(b, 0, 4)
                                cross_output(b, 1, 5)
                                if a is not None:
                                    pe.wait_ge(s1_masked, NB * (a + 1))
                                for j, to_bank in zip(range(4, 8), (6, 7, 3, 0)):
                                    cross_scores(j, to_bank)
                            if a is not None:
                                if b is not None:
                                    pe.wait_ge(o_lo, EC * b + 2)
                                value_rows(2, 4)
                                value_rows(3, 5)
                                pe.wait_ge(prob_ready, NB * (a + 1))
                                pe.wait_ge(v_lo, NB * a + 2)
                                for i in range(NB):
                                    last = pe.transpose(bank[1][:, cols(i)], prob[:, i, :], ident[:, :])
                                last.then_inc(pT_done, 1)
                            if b is not None:
                                cross_output(b, 2, 2)
                                cross_output(b, 3, 6)
                            if a is not None:
                                pe.wait_ge(pT_lo, a + 1)
                                pe.wait_ge(v_lo, NB * (a + 1))
                                for i in range(NB):
                                    product(pe, bank[BLOCK_BANK[i]][:, :], at(probT, cols(i)), at(yv, i), True, True
                                            ).then_inc(pv_done, 1)
                            if b is not None:
                                pe.wait_ge(o_lo, EC * (b + 1))
                                for i in range(NB):
                                    project(PROJ_BANK[i], lambda c: at(qo, c, cols(i)), lambda c: at(wo, c),
                                            proj_done)
                            if a is not None:
                                for i in range(NB):
                                    pe.wait_ge(z2_ready, NB * a + i + 1)
                                    transposed_rows(i, BLOCK_BANK[i], z2T_done)

                        pipeline(pe, step)

        feed = ExitStack()
        with feed:
            sb, pair, sem = names(feed)
            STAGES = 3
            w1p = pair("w1p", [P, EC, FF])
            w2p = pair("w2p", [P, FC, E])
            w1_raw = sb("w1_raw", [P, STAGES, EC, P])
            w2_raw = sb("w2_raw", [P, STAGES, E])
            b1_col = sb("b1_col", [P, FC])
            b2_row = sb("b2_row", [P, E])
            xc = sb("xc", [P, 2, NB, E])
            zn = sb("zn3", [P, NB, E])
            zT = pair("z3T", [P, EC, TILE])
            hid = pair("hid", [P, 4, TILE])
            gelu_out = sb("gelu_out", [P, 2, TILE])
            stats = sb("stats3", [P, NB, 6])
            mv, ve, rstd = sb("mv3", [P, NB, 2]), sb("ve3", [P, NB]), sb("rstd3", [P, NB])
            minus_half = sb("minus_half3", [P, NB])

            w1_loaded = [sem(f"w1_loaded{i}") for i in range(STAGES)]
            w2_loaded = [sem(f"w2_loaded{i}") for i in range(STAGES)]
            xc_loaded = [sem(f"xc_loaded{i}") for i in range(NB)]
            out_stored = [sem(f"out_stored{i}") for i in range(NB)]
            b_loaded, half3_set = sem("b_loaded"), sem("half3_set")
            w1_hi, w1_lo, w2_hi, w2_lo = sem("w1_hi"), sem("w1_lo"), sem("w2_hi"), sem("w2_lo")
            ln3_stats, ln3_mv, ln3_ve, ln3_rstd, z3_ready, xc_biased = (
                sem("ln3_stats"), sem("ln3_mv"), sem("ln3_ve"), sem("ln3_rstd"), sem("z3_ready"), sem("xc_biased"))
            z3T_done, z3T_hi, z3T_lo = sem("z3T_done"), sem("z3T_hi"), sem("z3T_lo")
            up_done, down_done, hid_full, hid_lo, out_ready = (
                sem("up_done"), sem("down_done"), sem("hid_full"), sem("hid_lo"), sem("out_ready"))

            def feed_tiles(engine, step):
                step(0, True, 0)
                with engine.Fori(0, (TILES - 2) // 2) as n:
                    for u in range(2):
                        step(2 * n + u + 1, True, 1 - u)
                step(TILES - 1, False, 1)

            def splits_weights(t):
                return isinstance(t, int) and t == 0

            with nc.Block() as block:
                @block.sync
                def _(sp):
                    def load_x(t, slot):
                        for i in range(NB):
                            sp.dma_start(xc[:, slot, i, :], x2_dram[t * NB + i, :, :]).then_inc(xc_loaded[i], 16)

                    def load_weights(c):
                        s = c % STAGES
                        if c >= STAGES:
                            sp.wait_ge(w1_lo, c - STAGES + 1)
                            sp.wait_ge(w2_lo, c - STAGES + 1)
                        sp.dma_start(w1_raw[:, s, :, :], w1[:, cols(c)].rearrange("(c p) n -> p c n", p=P)
                                     ).then_inc(w1_loaded[s], 16)
                        sp.dma_start(w2_raw[:, s, :], w2[cols(c), :]).then_inc(w2_loaded[s], 16)

                    def step(t, more, par):
                        if splits_weights(t):
                            load_x(0, 0)
                            load_weights(0)
                            sp.dma_start(b1_col[:, :], b1).then_inc(b_loaded, 16)
                            sp.dma_start(b2_row[:, :], b2.partition_broadcast(P)).then_inc(b_loaded, 16)
                            load_weights(1)
                            load_weights(2)
                            sp.wait_ge(ln3_stats, NB)
                            load_x(1, 1)
                            for c in range(3, FC):
                                load_weights(c)
                        elif more:
                            for i in range(NB):
                                sp.wait_ge(out_stored[i], 16 * t)
                            load_x(t + 1, 1 - par)
                        for i in range(NB):
                            sp.wait_ge(out_ready, NB * t + i + 1)
                            sp.dma_start(out_blocks[t * NB + i, :, :], xc[:, par, i, :]
                                         ).then_inc(out_stored[i], 16)

                    feed_tiles(sp, step)
                    for i in range(NB):
                        sp.wait_ge(out_stored[i], 16 * TILES)

                @block.gpsimd
                def _(pool):
                    def norm(t, slot):
                        pool.wait_ge(ln3_mv, NB * (t + 1))
                        pool.nop(nofuse=True)
                        pool.tensor_scalar(ve[:, :], mv[:, :, 1], LN_EPS, None, ALU.add).then_inc(ln3_ve, 1)
                        pool.wait_ge(ln3_ve, t + 1)
                        pool.tensor_tensor(rstd[:, :], ve[:, :], minus_half[:, :], ALU.pow).then_inc(ln3_rstd, 1)
                        pool.wait_ge(ln3_rstd, t + 1)
                        if not splits_weights(t):
                            pool.wait_ge(z3T_done, NB * t)
                        pool.nop(nofuse=True)
                        for i in range(NB):
                            pool.tensor_scalar(zn[:, i, :], xc[:, slot, i, :], mv[:, i, 0:1], rstd[:, i:i + 1],
                                               ALU.subtract, ALU.mult).then_inc(z3_ready, 1)
                        pool.wait_ge(z3_ready, NB * (t + 1))
                        for i in range(NB):
                            pool.tensor_tensor(xc[:, slot, i, :], xc[:, slot, i, :], b2_row[:, :], ALU.add
                                               ).then_inc(xc_biased, 1)

                    def split_w2(c):
                        s = c % STAGES
                        pool.wait_ge(w2_loaded[s], 16 * (c // STAGES + 1))
                        pool.tensor_copy(w2p[0][:, c, :], w2_raw[:, s, :]).then_inc(w2_hi, 1)
                        pool.wait_ge(w2_hi, c + 1)
                        pool.tensor_tensor(w2p[1][:, c, :], w2_raw[:, s, :], f(w2p[0][:, c, :]), ALU.subtract
                                           ).then_inc(w2_lo, 1)

                    def step(t, more, par):
                        for c in range(FC):
                            if splits_weights(t):
                                split_w2(c)
                            if c == 10 and more:
                                norm(t + 1, 1 - par)

                    pool.memset(minus_half[:, :], -0.5).then_inc(half3_set, 1)
                    pool.wait_ge(half3_set, 1)
                    pool.wait_ge(b_loaded, 32)
                    norm(0, 0)
                    feed_tiles(pool, step)

                @block.scalar
                def _(act):
                    def split_w1(c):
                        act.wait_ge(w1_loaded[c % STAGES], 16 * (c // STAGES + 1))
                        act.activation(w1p[0][:, :, cols(c)], w1_raw[:, c % STAGES, :, :], ACT.Copy
                                       ).then_inc(w1_hi, 1)

                    def z_high(t):
                        for i in range(NB):
                            act.wait_ge(z3T_done, NB * t + i + 1)
                            act.activation(zT[0][:, :, cols(i)], bank[LN3_BANK[i]][:, :].rearrange(
                                "p (c t) -> p c t", c=EC), ACT.Copy).then_inc(z3T_hi, 1)

                    def step(t, more, par):
                        for c in range(FC):
                            if splits_weights(t) and c + 2 < FC:
                                split_w1(c + 2)
                            act.wait_ge(up_done, FC * t + c + 1)
                            if c >= 4:
                                act.wait_ge(down_done, FC * t + c - 3)
                            act.activation(hid[0][:, c % 4, :], bank[4 + c % 3][:, :], ACT.Gelu,
                                           bias=b1_col[:, c:c + 1])
                            if c >= 2:
                                act.wait_ge(hid_lo, FC * t + c - 1)
                            act.activation(gelu_out[:, c % 2, :], bank[4 + c % 3][:, :], ACT.Gelu,
                                           bias=b1_col[:, c:c + 1]).then_inc(hid_full, 1)
                        if more:
                            z_high(t + 1)

                    split_w1(0)
                    split_w1(1)
                    act.wait_ge(b_loaded, 32)
                    z_high(0)
                    feed_tiles(act, step)

                @block.vector
                def _(dve):
                    def row_stats(t, slot):
                        for i in range(NB):
                            dve.wait_ge(xc_loaded[i], 16 * (t + 1))
                        dve.nop(nofuse=True)
                        for i in range(NB):
                            dve.bn_stats(stats[:, i, :], xc[:, slot, i, :]).then_inc(ln3_stats, 1)
                        dve.wait_ge(ln3_stats, NB * (t + 1))
                        dve.nop(nofuse=True)
                        for i in range(NB):
                            dve.bn_aggr(mv[:, i, :], stats[:, i, :]).then_inc(ln3_mv, 1)

                    def split_w1(c):
                        dve.wait_ge(w1_hi, c + 1)
                        dve.tensor_tensor(w1p[1][:, :, cols(c)], w1_raw[:, c % STAGES, :, :],
                                          f(w1p[0][:, :, cols(c)]), ALU.subtract).then_inc(w1_lo, 1)

                    def z_low(t):
                        for i in range(NB):
                            dve.wait_ge(z3T_hi, NB * t + i + 1)
                            dve.tensor_tensor(zT[1][:, :, cols(i)], bank[LN3_BANK[i]][:, :].rearrange(
                                "p (c t) -> p c t", c=EC), f(zT[0][:, :, cols(i)]), ALU.subtract
                                ).then_inc(z3T_lo, 1)

                    def step(t, more, par):
                        for c in range(FC):
                            if splits_weights(t) and c + 2 < FC:
                                split_w1(c + 2)
                            if c == 8 and more:
                                row_stats(t + 1, 1 - par)
                            dve.wait_ge(hid_full, FC * t + c + 1)
                            dve.tensor_tensor(hid[1][:, c % 4, :], gelu_out[:, c % 2, :], f(hid[0][:, c % 4, :]),
                                              ALU.subtract).then_inc(hid_lo, 1)
                        if more:
                            z_low(t + 1)
                        dve.wait_ge(xc_biased, NB * (t + 1))
                        dve.wait_ge(down_done, FC * (t + 1))
                        for i in range(NB):
                            dve.tensor_tensor(xc[:, par, i, :], bank[i][:, :], xc[:, par, i, :], ALU.add
                                              ).then_inc(out_ready, 1)

                    row_stats(0, 0)
                    split_w1(0)
                    split_w1(1)
                    z_low(0)
                    feed_tiles(dve, step)

                @block.tensor
                def _(pe):
                    def transposed_rows(t, i):
                        pe.wait_ge(z3_ready, NB * t + i + 1)
                        for c in range(EC):
                            last = pe.transpose(bank[LN3_BANK[i]][:, cols(c)], zn[:, i, cols(c)], ident[:, :])
                        last.then_inc(z3T_done, 1)

                    def up(t, c):
                        if splits_weights(t):
                            pe.wait_ge(w1_lo, c + 1)
                        if c >= 3:
                            pe.wait_ge(hid_full, FC * t + c - 2)
                        for k in range(EC):
                            last = product(pe, bank[4 + c % 3][:, :], at(w1p, k, cols(c)), at(zT, k),
                                           k == 0, k == EC - 1)
                        last.then_inc(up_done, 1)

                    def down(t, c):
                        if splits_weights(t):
                            pe.wait_ge(w2_lo, c + 1)
                        pe.wait_ge(hid_lo, FC * t + c + 1)
                        if c == 0 and not splits_weights(t):
                            pe.wait_ge(out_ready, NB * t)
                        for i in range(NB):
                            last = product(pe, bank[i][:, :], at(hid, c % 4, cols(i)), at(w2p, c),
                                           c == 0, c == FC - 1)
                        last.then_inc(down_done, 1)

                    def step(t, more, par):
                        pe.wait_ge(z3T_lo, NB * (t + 1))
                        for c in range(FC):
                            up(t, c)
                            if c >= 2:
                                down(t, c - 2)
                        if more:
                            transposed_rows(t + 1, 0)
                            pe.wait_ge(hid_full, FC * t + FC - 2)
                            transposed_rows(t + 1, 1)
                            pe.wait_ge(hid_full, FC * t + FC - 1)
                            transposed_rows(t + 1, 2)
                        down(t, FC - 2)
                        if more:
                            pe.wait_ge(hid_full, FC * (t + 1))
                            transposed_rows(t + 1, 3)
                        down(t, FC - 1)

                    for i in range(NB):
                        transposed_rows(0, i)
                    feed_tiles(pe, step)


def kernel(x, ctx_1024, mask_Bx1xSxS2_ik1, L0_attn_W_qkv, L0_attn_W_out, L0_attn_b_out, L0_xattn_Wq, L0_xattn_bq,
           L0_xattn_Wk, L0_xattn_bk, L0_xattn_Wv, L0_xattn_bv, L0_xattn_Wo, L0_ffn_w1, L0_ffn_b1, L0_ffn_w2,
           L0_ffn_b2):
    import numpy as np
    import concourse.bacc as bacc
    from concourse.bass_utils import run_bass_kernel_spmd

    def columns(v):
        return np.asarray(v).reshape(-1, P).T

    mask_tiles = np.asarray(mask_Bx1xSxS2_ik1).reshape(TILES, TILE, KEYS).transpose(0, 2, 1)
    laid_out = {
        "x": x, "ctxT": np.asarray(ctx_1024).transpose(2, 0, 1), "mask": mask_tiles,
        "wqkvT": np.asarray(L0_attn_W_qkv).T, "woutT": np.asarray(L0_attn_W_out).T, "b_out": L0_attn_b_out,
        "xwqT": np.asarray(L0_xattn_Wq).T, "bq": columns(L0_xattn_bq),
        "xwkT": np.asarray(L0_xattn_Wk).T, "bk": columns(L0_xattn_bk),
        "xwvT": np.asarray(L0_xattn_Wv).T, "bv": L0_xattn_bv, "xwoT": np.asarray(L0_xattn_Wo).T,
        "w1": L0_ffn_w1, "b1": columns(L0_ffn_b1), "w2": L0_ffn_w2, "b2": L0_ffn_b2,
    }
    nc = bacc.Bacc("TRN2", target_bir_lowering=False, num_devices=1)
    arrays, args = {}, []
    for name, value in laid_out.items():
        a = np.ascontiguousarray(value)
        arrays[f"in_{name}"] = a
        args.append(nc.dram_tensor(f"in_{name}", a.shape, mybir.dt.from_np(a.dtype), kind="ExternalInput").ap())
    args.append(nc.dram_tensor("out_dram", (BATCH, SEQ, E), mybir.dt.float32, kind="ExternalOutput").ap())
    decoder_layer_program(nc, *args)
    result = run_bass_kernel_spmd(nc, [arrays], core_ids=[0])
    return result.results[0]["out_dram"]
```

```python
import concourse.bass as bass
from concourse import mybir
from contextlib import ExitStack

P = 128
BATCH, SEQ, E = 4, 1024, 512
EC = E // P
TILE = 512
NB = TILE // P
TILES = BATCH * SEQ // TILE
TILES_PER_BATCH = SEQ // TILE
KEYS = 64
HEADS, HEAD_DIM = 16, 32
PAIRS = HEADS // 2
HEADS_PER_CHUNK = P // HEAD_DIM
FF = 2048
FC = FF // P
LN_EPS = 1e-5
DEN_EPS = 1e-6
SELF_SCALE = float(E) ** -0.5
CROSS_SCALE = float(HEAD_DIM) ** -0.5
MASKED = -3.0e38
STAGES = 3

VALUE_BANK = (1, 2, 3, 4)
SCORE_BANK = (0, 1, 2, 3, 5, 6, 7, 0)
OUT_BANK = (3, 4, 5, 1)
BLOCK_BANK = (6, 7, 0, 2)
PROJ_BANK = (3, 4, 5, 1)
FIRST_BANK = (4, 5, 6, 7)
LN3_BANK = (7, 5, 6, 4)


def decoder_layer_program(nc, x, ctxT, mask, wqkvT, woutT, b_out, xwqT, bq, xwkT, bk, xwvT, bv, xwoT,
                          w1, b1, w2, b2, out):
    fp32, fp32r, i32 = mybir.dt.float32, mybir.dt.float32r, mybir.dt.int32
    ALU, ACT, AX = mybir.AluOpType, mybir.ActivationFunctionType, mybir.AxisListType

    def product(pe, out_ap, lhs, rhs, start, stop):
        pe.matmul(out_ap, lhs[1], rhs[0], start=start, stop=False)
        pe.matmul(out_ap, lhs[0], rhs[1], start=False, stop=False)
        return pe.matmul(out_ap, lhs[0], rhs[0], start=False, stop=stop)

    def f(ap):
        return ap.bitcast(fp32)

    def cols(n, width=P):
        return slice(n * width, (n + 1) * width)

    x_blocks = x.rearrange("b (n p) e -> (b n) p e", p=P)
    out_blocks = out.rearrange("b (n p) e -> (b n) p e", p=P)
    x2_dram = nc.dram_tensor("x2_dram", (TILES * NB, P, E), fp32).ap()
    keys_dram = nc.dram_tensor("keys_dram", (BATCH, P, EC * KEYS), fp32).ap()
    values_dram = nc.dram_tensor("values_dram", (BATCH, P, E), fp32).ap()

    whole = ExitStack()
    with whole:
        def names(stack):
            def sb(name, shape, dt=fp32):
                return stack.enter_context(nc.sbuf_tensor(name, shape, dt))

            def pair(name, shape):
                return sb(name + "_hi", shape, fp32r), sb(name + "_lo", shape, fp32r)

            def sem(name):
                return stack.enter_context(nc.semaphore(name))
            return sb, pair, sem

        def at(hl, *index):
            return tuple(part[(slice(None),) + index] for part in hl)

        sb, pair, sem = names(whole)
        bank = [whole.enter_context(nc.psum_tensor(f"bank{i}", [P, TILE], fp32)) for i in range(8)]
        ident = sb("ident", [P, P])
        resid = sb("resid", [P, 2, NB, E])
        zn = sb("zn", [P, NB, E])
        zT = pair("zT", [P, EC, TILE])
        w1_raw = sb("w1_raw", [P, STAGES, EC, P])
        w2_raw = sb("w2_raw", [P, STAGES, E])
        stats = sb("stats", [P, NB, 6])
        mv1, mv2, mv3 = sb("mv1", [P, NB, 2]), sb("mv2", [P, NB, 2]), sb("mv3", [P, NB, 2])
        ve1, ve2, ve3 = sb("ve1", [P, NB]), sb("ve2", [P, NB]), sb("ve3", [P, NB])
        rstd1, rstd2, rstd3 = sb("rstd1", [P, NB]), sb("rstd2", [P, NB]), sb("rstd3", [P, NB])
        minus_half = sb("minus_half", [P, NB])

        x_loaded = [sem(f"x_loaded{i}") for i in range(NB)]
        x2_stored = [sem(f"x2_stored{i}") for i in range(NB)]
        x2_loaded = [sem(f"x2_loaded{i}") for i in range(NB)]
        w1_loaded = [sem(f"w1_loaded{i}") for i in range(STAGES)]
        w2_loaded = [sem(f"w2_loaded{i}") for i in range(STAGES)]
        ln1, ln2, ln3 = (tuple(sem(f"{n}_{what}") for what in ("stats", "mv", "ve", "rstd", "ready"))
                         for n in ("ln1", "ln2", "ln3"))
        z1_ready, z2_ready, z3_ready = ln1[4], ln2[4], ln3[4]
        z1T_done, z1T_hi, z1T_lo = sem("z1T_done"), sem("z1T_hi"), sem("z1T_lo")
        z2T_done, z2T_hi, z2T_lo = sem("z2T_done"), sem("z2T_hi"), sem("z2T_lo")
        z3T_done, z3T_hi, z3T_lo = sem("z3T_done"), sem("z3T_hi"), sem("z3T_lo")
        filled = sem("filled")

        def chunks(ap):
            return ap.rearrange("p (c t) -> p c t", c=EC)

        def norm_stats(dve, rows_of, mv, ln, t):
            for i in range(NB):
                dve.bn_stats(stats[:, i, :], rows_of(i)).then_inc(ln[0], 1)
            dve.wait_ge(ln[0], NB * (t + 1))
            dve.nop(nofuse=True)
            for i in range(NB):
                dve.bn_aggr(mv[:, i, :], stats[:, i, :]).then_inc(ln[1], 1)

        def norm_rstd(pool, mv, ve, rstd, ln, t):
            pool.wait_ge(ln[1], NB * (t + 1))
            pool.nop(nofuse=True)
            pool.tensor_scalar(ve[:, :], mv[:, :, 1], LN_EPS, None, ALU.add).then_inc(ln[2], 1)
            pool.wait_ge(ln[2], t + 1)
            pool.tensor_tensor(rstd[:, :], ve[:, :], minus_half[:, :], ALU.pow).then_inc(ln[3], 1)

        def norm_rows(dve, rows_of, mv, rstd, ln, t):
            dve.wait_ge(ln[3], t + 1)
            for i in range(NB):
                dve.tensor_scalar(zn[:, i, :], rows_of(i), mv[:, i, 0:1], rstd[:, i:i + 1],
                                  ALU.subtract, ALU.mult).then_inc(ln[4], 1)

        def transposed_rows(pe, ready, t, i, to_bank, done):
            pe.wait_ge(ready, NB * t + i + 1)
            for c in range(EC):
                last = pe.transpose(bank[to_bank][:, cols(c)], zn[:, i, cols(c)], ident[:, :])
            last.then_inc(done, 1)

        def transpose_high(act, i, from_bank, done, made, t):
            act.wait_ge(done, NB * t + i + 1)
            act.activation(zT[0][:, :, cols(i)], chunks(bank[from_bank][:, :]), ACT.Copy).then_inc(made, 1)

        def transpose_low(dve, i, from_bank, hi_made, made, t):
            dve.wait_ge(hi_made, NB * t + i + 1)
            dve.tensor_tensor(zT[1][:, :, cols(i)], chunks(bank[from_bank][:, :]), f(zT[0][:, :, cols(i)]),
                              ALU.subtract).then_inc(made, 1)

        def load_ff_weights(sp, c):
            s = c % STAGES
            sp.dma_start(w1_raw[:, s, :, :], w1[:, cols(c)].rearrange("(c p) n -> p c n", p=P)
                         ).then_inc(w1_loaded[s], 16)
            sp.dma_start(w2_raw[:, s, :], w2[cols(c), :]).then_inc(w2_loaded[s], 16)

        def load_x2(sp, t, slot, i):
            sp.dma_start(resid[:, slot, i, :], x2_dram[t * NB + i, :, :]).then_inc(x2_loaded[i], 16)

        layer = ExitStack()
        with layer:
            sb, pair, sem = names(layer)
            wqk = pair("wqk", [P, EC, E])
            wvo = pair("wvo", [P, EC, E])
            wq = pair("wq", [P, EC, E])
            wo = pair("wo", [P, EC, E])
            x_in = sb("x_in", [P, NB, E])
            bq_col = sb("bq_col", [P, EC])
            bout_row = sb("bout_row", [P, E])
            causal = sb("causal", [P, P])
            kb = pair("kb", [P, EC, P])
            vb = pair("vb", [P, PAIRS, P])

            kv_stored = sem("kv_stored")

            def load_x(sp, t, i):
                sp.dma_start(x_in[:, i, :], x_blocks[t * NB + i, :, :]).then_inc(x_loaded[i], 16)

            setup = ExitStack()
            with setup:
                sb, pair, sem = names(setup)
                RAWS, PARTS = 2 * NB, 8
                part = pair("part", [P, PARTS, E])
                ctx_raw = sb("ctx_raw", [P, EC, BATCH, KEYS])
                ctx2 = pair("ctx2", [P, EC, BATCH, 2, KEYS])
                keysT = sb("keysT", [P, BATCH, EC, KEYS])
                values = sb("values", [P, BATCH, E])
                bk_col = sb("bk_col", [P, EC])
                bv_row = sb("bv_row", [P, E])

                raw_loaded = [sem(f"raw_loaded{i}") for i in range(RAWS)]
                ctx_loaded, bias_loaded = sem("ctx_loaded"), sem("bias_loaded")
                split_hi, split_lo, split_lo_pool = sem("split_hi"), sem("split_lo"), sem("split_lo_pool")
                ctx_hi, ctx_lo = sem("ctx_hi"), sem("ctx_lo")
                shaped, part_used = sem("shaped"), sem("part_used")
                wqk_done, wvo_done, keys_done, values_done = (
                    sem("wqk_done"), sem("wvo_done"), sem("keys_done"), sem("values_done"))
                wqk_hi, wqk_lo, wvo_hi, wvo_lo = sem("wqk_hi"), sem("wqk_lo"), sem("wvo_hi"), sem("wvo_lo")
                keys_out, values_out = sem("keys_out"), sem("values_out")

                def raw(n):
                    return resid[:, n % RAWS // NB, n % NB, :]

                CHUNKS = [wqkvT[h * E + c * P:h * E + (c + 1) * P, :] for c in range(EC) for h in (0, 1)]
                for c in range(EC):
                    CHUNKS += [wqkvT[2 * E + c * P:2 * E + (c + 1) * P, :], woutT[cols(c), :]]
                CHUNKS += [w[cols(c), :] for w in (xwkT, xwvT, xwqT, xwoT) for c in range(EC)]
                FOLDED = 24
                TARGET = [at(part, n % PARTS) for n in range(FOLDED)]
                TARGET += [at(w, c) for w in (wq, wo) for c in range(EC)]

                with nc.Block() as block:
                    @block.sync
                    def _(sp):
                        for n, w in enumerate(CHUNKS):
                            if n >= RAWS:
                                sp.wait_ge(split_lo, n - RAWS + 1)
                            sp.dma_start(raw(n), w).then_inc(raw_loaded[n % RAWS], 16)
                            if n == RAWS - 1:
                                sp.dma_start(ctx_raw[:, :, :, :], ctxT.rearrange("(c p) b k -> p c b k", p=P)
                                             ).then_inc(ctx_loaded, 16)
                                for i in range(NB):
                                    load_x(sp, 0, i)
                                sp.dma_start(bk_col[:, :], bk).then_inc(bias_loaded, 16)
                                sp.dma_start(bq_col[:, :], bq).then_inc(bias_loaded, 16)
                                sp.dma_start(bv_row[:, :], bv.partition_broadcast(P)).then_inc(bias_loaded, 16)
                                sp.dma_start(bout_row[:, :], b_out.partition_broadcast(P)).then_inc(bias_loaded, 16)
                        sp.wait_ge(keys_out, EC)
                        sp.dma_start(keys_dram.rearrange("b p n -> p b n"),
                                     keysT[:, :, :, :].rearrange("p b c k -> p b (c k)")).then_inc(kv_stored, 16)
                        sp.wait_ge(values_out, BATCH)
                        sp.dma_start(values_dram.rearrange("b p n -> p b n"), values[:, :, :]
                                     ).then_inc(kv_stored, 16)

                    @block.scalar
                    def _(act):
                        def split_high(n):
                            act.wait_ge(raw_loaded[n % RAWS], 16 * (n // RAWS + 1))
                            if PARTS <= n < FOLDED:
                                act.wait_ge(part_used, (n - PARTS) // 2 + 1)
                            act.activation(TARGET[n][0], raw(n), ACT.Copy).then_inc(split_hi, 1)

                        def evacuate_high(hl, banks, done, made):
                            act.wait_ge(done, 1)
                            for m in range(EC):
                                act.activation(hl[0][:, m, :], bank[banks + m][:, :], ACT.Copy).then_inc(made, 1)

                        for n in range(8):
                            split_high(n)
                        act.wait_ge(ctx_loaded, 16)
                        for d in range(2):
                            act.activation(ctx2[0][:, :, :, d, :], ctx_raw[:, :, :, :], ACT.Copy
                                           ).then_inc(ctx_hi, 1)
                        for n in range(8, 16):
                            split_high(n)
                        evacuate_high(wqk, 0, wqk_done, wqk_hi)
                        for n in range(16, 24):
                            split_high(n)
                        evacuate_high(wvo, 4, wvo_done, wvo_hi)
                        for n in range(24, 32):
                            split_high(n)
                        act.wait_ge(bias_loaded, 64)
                        act.wait_ge(keys_done, 1)
                        for m in range(EC):
                            act.activation(keysT[:, :, m, :], bank[m][:, 0:BATCH * KEYS].rearrange(
                                "p (b k) -> p b k", b=BATCH), ACT.Identity, bias=bk_col[:, m:m + 1]
                                ).then_inc(keys_out, 1)
                        for i in range(NB):
                            transpose_high(act, i, i, z1T_done, z1T_hi, 0)

                    @block.vector
                    def _(dve):
                        def split_low(n):
                            dve.wait_ge(split_hi, n + 1)
                            dve.tensor_tensor(TARGET[n][1], raw(n), f(TARGET[n][0]), ALU.subtract
                                              ).then_inc(split_lo, 1)

                        def evacuate_low(hl, banks, hi, made):
                            for m in range(EC):
                                dve.wait_ge(hi, m + 1)
                                dve.tensor_tensor(hl[1][:, m, :], bank[banks + m][:, :], f(hl[0][:, m, :]),
                                                  ALU.subtract).then_inc(made, 1)

                        for n in range(8):
                            split_low(n)
                        for d in range(2):
                            dve.wait_ge(ctx_hi, d + 1)
                            dve.tensor_tensor(ctx2[1][:, :, :, d, :], ctx_raw[:, :, :, :],
                                              f(ctx2[0][:, :, :, d, :]), ALU.subtract).then_inc(ctx_lo, 1)
                        for n in range(8, 16):
                            split_low(n)
                        evacuate_low(wqk, 0, wqk_hi, wqk_lo)
                        for n in range(16, 24):
                            split_low(n)
                        evacuate_low(wvo, 4, wvo_hi, wvo_lo)
                        for i in range(NB):
                            dve.wait_ge(x_loaded[i], 16)
                        norm_stats(dve, lambda i: x_in[:, i, :], mv1, ln1, 0)
                        norm_rows(dve, lambda i: x_in[:, i, :], mv1, rstd1, ln1, 0)
                        dve.wait_ge(bias_loaded, 64)
                        dve.wait_ge(values_done, 1)
                        for b in range(BATCH):
                            dve.tensor_tensor(values[:, b, :], bank[4 + b][:, :], bv_row[:, :], ALU.add
                                              ).then_inc(values_out, 1)
                        for i in range(NB):
                            transpose_low(dve, i, i, z1T_hi, z1T_lo, 0)

                    @block.gpsimd
                    def _(pool):
                        pool.memset(ident[:, :], 0.0).then_inc(filled, 1)
                        pool.memset(causal[:, :], 0.0).then_inc(filled, 1)
                        pool.memset(minus_half[:, :], -0.5).then_inc(filled, 1)
                        for part_ in (*kb, *vb):
                            pool.memset(f(part_[:, :, :]), 0.0).then_inc(filled, 1)
                        pool.wait_ge(filled, 7)
                        pool.affine_select(out=ident[:, :], in_=ident[:, :], compare_op=ALU.not_equal, fill=1.0,
                                           base=0, pattern=[[-1, P]], channel_multiplier=1).then_inc(shaped, 1)
                        pool.affine_select(out=causal[:, :], in_=causal[:, :], compare_op=ALU.is_ge, fill=MASKED,
                                           base=0, pattern=[[-1, P]], channel_multiplier=1).then_inc(shaped, 1)
                        norm_rstd(pool, mv1, ve1, rstd1, ln1, 0)
                        for n in range(FOLDED, len(CHUNKS)):
                            pool.wait_ge(split_hi, n + 1)
                            pool.tensor_tensor(TARGET[n][1], raw(n), f(TARGET[n][0]), ALU.subtract
                                               ).then_inc(split_lo_pool, 1)
                        pool.wait_ge(shaped, 2)
                        pool.wait_ge(split_lo_pool, len(CHUNKS) - FOLDED)

                    @block.tensor
                    def _(pe):
                        def fold(first_chunk, banks, done):
                            for c in range(EC):
                                n = first_chunk + 2 * c
                                pe.wait_ge(split_lo, n + 2)
                                for m in range(EC):
                                    last = product(pe, bank[banks + m][:, :], at(part, n % PARTS, cols(m)),
                                                   at(part, (n + 1) % PARTS), c == 0, c == EC - 1)
                                last.then_inc(part_used if c < EC - 1 else done, 1)
                                if c == EC - 1:
                                    pe.wait_ge(done, 1)
                                    pe.sem_inc(part_used, 1)

                        fold(0, 0, wqk_done)
                        fold(8, 4, wvo_done)
                        pe.wait_ge(ctx_lo, 2)
                        pe.wait_ge(wqk_lo, EC)
                        for c in range(EC):
                            pe.wait_ge(split_lo, 16 + c + 1)
                            for m in range(EC):
                                last = product(pe, bank[m][:, 0:BATCH * KEYS], at(part, (16 + c) % PARTS, cols(m)),
                                               at(ctx2, c, slice(None), 0), c == 0, c == EC - 1)
                        last.then_inc(keys_done, 1)
                        pe.wait_ge(wvo_lo, EC)
                        for c in range(EC):
                            pe.wait_ge(split_lo, 20 + c + 1)
                            for b in range(BATCH):
                                last = product(pe, bank[4 + b][:, :], at(ctx2, c, b), at(part, (20 + c) % PARTS),
                                               c == 0, c == EC - 1)
                        last.then_inc(values_done, 1)
                        pe.wait_ge(shaped, 2)
                        pe.wait_ge(keys_out, EC)
                        for i in range(NB):
                            transposed_rows(pe, z1_ready, 0, i, i, z1T_done)

            both = ExitStack()
            with both:
                sb, pair, sem = names(both)
                yv = pair("yv", [P, EC, TILE])
                qo = pair("qo", [P, EC, TILE])
                attn = pair("attn", [P, 4, TILE])
                act_in = sb("act_in", [P, 3, TILE])
                mask_i = sb("mask_i", [P, TILE], i32)
                mask_f = sb("mask_f", [P, TILE])
                keys_now = sb("keys_now", [P, EC, KEYS])
                values_now = sb("values_now", [P, E])
                prob = sb("prob", [P, NB, P])
                probT = pair("probT", [P, TILE])
                nmax, nbias = sb("nmax", [P, NB]), sb("nbias", [P, NB])
                sums, den, rden = sb("sums", [P, NB]), sb("den", [P, NB]), sb("rden", [P, NB])

                mask_loaded, mask_ready = sem("mask_loaded"), sem("mask_ready")
                y_done, s1_done, v_done, pT_done, pv_done = (
                    sem("y_done"), sem("s1_done"), sem("v_done"), sem("pT_done"), sem("pv_done"))
                q_done, s2_done, o_done, proj_done = sem("q_done"), sem("s2_done"), sem("o_done"), sem("proj_done")
                y_hi, v_hi, pT_hi, q_hi, o_hi = sem("y_hi"), sem("v_hi"), sem("pT_hi"), sem("q_hi"), sem("o_hi")
                y_lo, v_lo, pT_lo, q_lo, o_lo = sem("y_lo"), sem("v_lo"), sem("pT_lo"), sem("q_lo"), sem("o_lo")
                s1_masked, s1_max, s1_bias, s1_exp, s1_den, s1_rden, prob_ready = (
                    sem("s1_masked"), sem("s1_max"), sem("s1_bias"), sem("s1_exp"), sem("s1_den"),
                    sem("s1_rden"), sem("prob_ready"))
                s2_masked, attn_full, attn_lo = sem("s2_masked"), sem("attn_full"), sem("attn_lo")
                kv_loaded, kv_hi, kv_ready = sem("kv_loaded"), sem("kv_hi"), sem("kv_ready")
                x_biased, x1_ready, x2_ready = sem("x_biased"), sem("x1_ready"), sem("x2_ready")

                BLOCKS = []
                for h in range(HEADS_PER_CHUNK):
                    r = cols(h, HEAD_DIM)
                    BLOCKS.append((tuple(k[r, :, cols(h % 2, KEYS)] for k in kb), keys_now[r, :, :]))
                for h in range(HEADS_PER_CHUNK):
                    r = cols(h % 2, KEYS)
                    BLOCKS.append((
                        tuple(v[r, :, :].rearrange("p (m o) n -> p m o n", o=2)[:, :, h // 2, cols(h, HEAD_DIM)]
                              for v in vb),
                        values_now[r, :].rearrange("p (m h e) -> p m h e", m=EC, e=HEAD_DIM)[:, :, h, :]))

                def pipeline(engine, step):
                    step(0, None, 0)
                    step(1, 0, 1)
                    with engine.Fori(0, (TILES - 2) // 2) as n:
                        for u in range(2):
                            step(2 * n + u + 2, 2 * n + u + 1, u)
                    step(None, TILES - 1, 0)

                def first(t):
                    return isinstance(t, int) and t == 0

                with nc.Block() as block:
                    @block.sync
                    def _(sp):
                        def load_mask(t):
                            for d in range(2):
                                sp.dma_start(mask_i[d * KEYS:(d + 1) * KEYS, :], mask[t, :, :]
                                             ).then_inc(mask_loaded, 16)

                        def load_kv(t):
                            batch = t // TILES_PER_BATCH
                            sp.dma_start(keys_now[:, :, :].rearrange("p c k -> p (c k)"), keys_dram[batch, :, :]
                                         ).then_inc(kv_loaded, 16)
                            sp.dma_start(values_now[:, :], values_dram[batch, :, :]).then_inc(kv_loaded, 16)

                        sp.wait_ge(kv_stored, 32)
                        load_kv(0)
                        load_mask(0)
                        with sp.Fori(0, TILES - 1) as t:
                            for i in range(NB):
                                sp.wait_ge(x1_ready, NB * t + i + 1)
                                load_x(sp, t + 1, i)
                            sp.wait_ge(kv_ready, len(BLOCKS) * (t + 1))
                            load_kv(t + 1)
                            sp.wait_ge(mask_ready, t + 1)
                            load_mask(t + 1)
                        for i in range(NB):
                            sp.wait_ge(x1_ready, NB * (TILES - 1) + i + 1)
                            sp.dma_start(x_in[:, i, :], x2_dram[i, :, :]).then_inc(x_loaded[i], 16)
                        for c in range(STAGES):
                            load_ff_weights(sp, c)

                    @block.gpsimd
                    def _(pool):
                        def silu_low(b, j):
                            pool.wait_ge(attn_full, PAIRS * b + j + 1)
                            pool.tensor_tensor(attn[1][:, j % 4, :], act_in[:, j % 3, :], f(attn[0][:, j % 4, :]),
                                               ALU.subtract).then_inc(attn_lo, 1)

                        def step(a, b, par):
                            if a is not None and not first(a):
                                norm_rstd(pool, mv1, ve1, rstd1, ln1, a)
                            if a is None:
                                norm_rstd(pool, mv3, ve3, rstd3, ln3, 0)
                            if b is not None:
                                for j in range(4):
                                    silu_low(b, j)
                            if a is not None:
                                pool.wait_ge(z1_ready, NB * (a + 1))
                                for i in range(NB):
                                    pool.tensor_tensor(x_in[:, i, :], x_in[:, i, :], bout_row[:, :], ALU.add
                                                       ).then_inc(x_biased, 1)
                            if b is not None:
                                for j in range(4, 8):
                                    silu_low(b, j)
                            if a is not None:
                                norm_rstd(pool, mv2, ve2, rstd2, ln2, a)

                        pipeline(pool, step)

                    @block.scalar
                    def _(act):
                        def y_high(a, m):
                            act.wait_ge(y_done, EC * a + m + 1)
                            act.activation(yv[0][:, m, :], bank[4 + m][:, :], ACT.Copy).then_inc(y_hi, 1)

                        def v_high(a, i):
                            act.wait_ge(v_done, NB * a + i + 1)
                            act.activation(yv[0][:, i, :], bank[VALUE_BANK[i]][:, :], ACT.Copy).then_inc(v_hi, 1)

                        def o_high(b, m):
                            act.wait_ge(o_done, EC * b + m + 1)
                            act.activation(qo[0][:, m, :], bank[OUT_BANK[m]][:, :], ACT.Copy).then_inc(o_hi, 1)

                        def silu(b, j):
                            act.wait_ge(s2_masked, PAIRS * b + j + 1)
                            act.activation(attn[0][:, j % 4, :], act_in[:, j % 3, :], ACT.Silu)
                            act.activation(act_in[:, j % 3, :], act_in[:, j % 3, :], ACT.Silu
                                           ).then_inc(attn_full, 1)

                        def step(a, b, par):
                            if b is not None:
                                act.wait_ge(kv_loaded, 32 * (b + 1))
                                for (hi, _), source in BLOCKS:
                                    act.activation(hi, source, ACT.Copy).then_inc(kv_hi, 1)
                                for m in range(EC):
                                    act.wait_ge(q_done, EC * b + m + 1)
                                    act.activation(qo[0][:, m, :], bank[m][:, :], ACT.Identity,
                                                   bias=bq_col[:, m:m + 1]).then_inc(q_hi, 1)
                            if a is not None and not first(a):
                                for i in range(NB):
                                    transpose_high(act, i, 4 + i, z1T_done, z1T_hi, a)
                            if b is not None:
                                for j in range(4):
                                    silu(b, j)
                            if a is not None:
                                for m in range(EC):
                                    y_high(a, m)
                                act.wait_ge(s1_bias, a + 1)
                                for i in range(NB):
                                    act.activation(prob[:, i, :], prob[:, i, :], ACT.Exp, bias=nbias[:, i:i + 1],
                                                   scale=SELF_SCALE, accum_out=sums[:, i:i + 1]
                                                   ).then_inc(s1_exp, 1)
                                v_high(a, 0)
                                v_high(a, 1)
                            if b is not None:
                                if a is None:
                                    for i in range(NB):
                                        transpose_high(act, i, FIRST_BANK[i], z3T_done, z3T_hi, 0)
                                o_high(b, 0)
                                o_high(b, 1)
                                silu(b, 4)
                                silu(b, 5)
                            if a is not None:
                                act.wait_ge(pT_done, a + 1)
                                act.activation(probT[0][:, :], bank[1][:, :], ACT.Copy).then_inc(pT_hi, 1)
                            if b is not None:
                                silu(b, 6)
                                silu(b, 7)
                            if a is not None:
                                v_high(a, 2)
                                v_high(a, 3)
                            if b is not None:
                                o_high(b, 2)
                                o_high(b, 3)
                            if a is not None:
                                for i in range(NB):
                                    transpose_high(act, i, BLOCK_BANK[i], z2T_done, z2T_hi, a)
                            if b is not None:
                                for i in range(NB):
                                    act.wait_ge(x2_ready, NB * b + i + 1)
                                    act.dma_start(x2_dram[b * NB + i, :, :], resid[:, 1 - par, i, :]
                                                  ).then_inc(x2_stored[i], 16)

                        act.wait_ge(kv_stored, 32)
                        pipeline(act, step)

                    @block.vector
                    def _(dve):
                        def low(hl, m, from_bank, hi_made, made, value):
                            dve.wait_ge(hi_made, value)
                            dve.tensor_tensor(hl[1][:, m, :], bank[from_bank][:, :], f(hl[0][:, m, :]),
                                              ALU.subtract).then_inc(made, 1)

                        def v_low(a, i):
                            low(yv, i, VALUE_BANK[i], v_hi, v_lo, NB * a + i + 1)

                        def o_low(b, m):
                            low(qo, m, OUT_BANK[m], o_hi, o_lo, EC * b + m + 1)

                        def q_low(b, m):
                            dve.wait_ge(q_hi, EC * b + m + 1)
                            dve.scalar_tensor_tensor(qo[1][:, m, :], bank[m][:, :], bq_col[:, m:m + 1],
                                                     f(qo[0][:, m, :]), ALU.add, ALU.subtract).then_inc(q_lo, 1)

                        def mask_scores(b, j):
                            dve.wait_ge(s2_done, PAIRS * b + j + 1)
                            if j >= 3:
                                dve.wait_ge(attn_lo, PAIRS * b + j - 2)
                            dve.scalar_tensor_tensor(act_in[:, j % 3, :], bank[SCORE_BANK[j]][:, :], CROSS_SCALE,
                                                     mask_f[:, :], ALU.mult, ALU.mult).then_inc(s2_masked, 1)

                        def x1_rows(i, par):
                            return resid[:, par, i, :]

                        def step(a, b, par):
                            if a is not None and not first(a):
                                for i in range(NB):
                                    dve.wait_ge(x_loaded[i], 16 * (a + 1))
                                dve.nop(nofuse=True)
                                norm_stats(dve, lambda i: x_in[:, i, :], mv1, ln1, a)
                            if a is None:
                                for i in range(NB):
                                    dve.wait_ge(x_loaded[i], 16 * (TILES + 1))
                                norm_stats(dve, lambda i: x_in[:, i, :], mv3, ln3, 0)
                            if b is not None:
                                dve.wait_ge(mask_loaded, 32 * (b + 1))
                                dve.tensor_scalar(mask_f[:, :], mask_i[:, :], 0.0, None, ALU.not_equal
                                                  ).then_inc(mask_ready, 1)
                                dve.wait_ge(kv_hi, len(BLOCKS) * (b + 1))
                                for (hi, lo), source in BLOCKS:
                                    dve.tensor_tensor(lo, source, f(hi), ALU.subtract).then_inc(kv_ready, 1)
                                q_low(b, 0)
                                q_low(b, 1)
                            if a is not None and not first(a):
                                dve.wait_ge(z2T_done, NB * a)
                                norm_rows(dve, lambda i: x_in[:, i, :], mv1, rstd1, ln1, a)
                            if a is None:
                                dve.wait_ge(z2T_done, NB * TILES)
                                norm_rows(dve, lambda i: x_in[:, i, :], mv3, rstd3, ln3, 0)
                            if b is not None:
                                q_low(b, 2)
                                q_low(b, 3)
                            if a is not None and not first(a):
                                for i in range(NB):
                                    transpose_low(dve, i, 4 + i, z1T_hi, z1T_lo, a)
                            if b is not None:
                                dve.wait_ge(mask_ready, b + 1)
                                for j in range(4):
                                    mask_scores(b, j)
                            if a is not None:
                                for m in range(EC):
                                    low(yv, m, 4 + m, y_hi, y_lo, EC * a + m + 1)
                                dve.wait_ge(s1_done, a + 1)
                                for i in range(NB):
                                    dve.tensor_tensor(prob[:, i, :], bank[0][:, cols(i)], causal[:, :], ALU.add
                                                      ).then_inc(s1_masked, 1)
                                dve.wait_ge(s1_masked, NB * (a + 1))
                                dve.reduce_max(nmax[:, :], prob[:, :, :], AX.X, negate=True).then_inc(s1_max, 1)
                                dve.wait_ge(s1_max, a + 1)
                                dve.tensor_scalar(nbias[:, :], nmax[:, :], SELF_SCALE, None, ALU.mult
                                                  ).then_inc(s1_bias, 1)
                                v_low(a, 0)
                                v_low(a, 1)
                                dve.wait_ge(s1_exp, NB * (a + 1))
                                dve.tensor_scalar(den[:, :], sums[:, :], DEN_EPS, None, ALU.add).then_inc(s1_den, 1)
                                dve.wait_ge(s1_den, a + 1)
                                dve.reciprocal(rden[:, :], den[:, :]).then_inc(s1_rden, 1)
                                dve.wait_ge(s1_rden, a + 1)
                                for i in range(NB):
                                    dve.tensor_scalar(prob[:, i, :], prob[:, i, :], rden[:, i:i + 1], None, ALU.mult
                                                      ).then_inc(prob_ready, 1)
                            else:
                                for i in range(NB):
                                    transpose_low(dve, i, FIRST_BANK[i], z3T_hi, z3T_lo, 0)
                            if b is not None:
                                o_low(b, 0)
                                o_low(b, 1)
                                for j in range(4, 7):
                                    mask_scores(b, j)
                            if a is not None:
                                dve.wait_ge(pT_hi, a + 1)
                                dve.tensor_tensor(probT[1][:, :], bank[1][:, :], f(probT[0][:, :]), ALU.subtract
                                                  ).then_inc(pT_lo, 1)
                            if b is not None:
                                mask_scores(b, 7)
                            if a is not None:
                                v_low(a, 2)
                                v_low(a, 3)
                                dve.wait_ge(x_biased, NB * (a + 1))
                                for i in range(NB):
                                    dve.wait_ge(pv_done, NB * a + i + 1)
                                    if b is not None and not first(b):
                                        dve.wait_ge(x2_stored[i], 16 * b)
                                    dve.tensor_tensor(x1_rows(i, par), bank[BLOCK_BANK[i]][:, :], x_in[:, i, :],
                                                      ALU.add).then_inc(x1_ready, 1)
                                dve.wait_ge(x1_ready, NB * (a + 1))
                                dve.nop(nofuse=True)
                                for i in range(NB):
                                    if b is not None and i >= 2:
                                        o_low(b, i)
                                    dve.bn_stats(stats[:, i, :], x1_rows(i, par)).then_inc(ln2[0], 1)
                                dve.wait_ge(ln2[0], NB * (a + 1))
                                dve.nop(nofuse=True)
                                for i in range(NB):
                                    dve.bn_aggr(mv2[:, i, :], stats[:, i, :]).then_inc(ln2[1], 1)
                                norm_rows(dve, lambda i: x1_rows(i, par), mv2, rstd2, ln2, a)
                            else:
                                o_low(b, 2)
                                o_low(b, 3)

                            def second_residual(i):
                                dve.wait_ge(proj_done, NB * b + i + 1)
                                dve.tensor_tensor(resid[:, 1 - par, i, :], bank[PROJ_BANK[i]][:, :],
                                                  resid[:, 1 - par, i, :], ALU.add).then_inc(x2_ready, 1)

                            if b is not None:
                                for i in range(3):
                                    second_residual(i)
                            if a is not None:
                                for i in range(NB):
                                    transpose_low(dve, i, BLOCK_BANK[i], z2T_hi, z2T_lo, a)
                            if b is not None:
                                second_residual(3)

                        dve.wait_ge(kv_stored, 32)
                        pipeline(dve, step)

                    @block.tensor
                    def _(pe):
                        def project(to_bank, lhs, rhs, done):
                            for c in range(EC):
                                last = product(pe, bank[to_bank][:, :], lhs(c), rhs(c), c == 0, c == EC - 1)
                            last.then_inc(done, 1)

                        def value_rows(i):
                            project(VALUE_BANK[i], lambda c: at(zT, c, cols(i)), lambda c: at(wvo, c), v_done)

                        def cross_scores(m):
                            rows = [cols(n, 2 * HEAD_DIM) for n in range(2)]
                            for hl_k, hl_q in ((1, 0), (0, 1), (0, 0)):
                                for n, r in enumerate(rows):
                                    last = pe.matmul(bank[SCORE_BANK[2 * m + n]][:, :], kb[hl_k][r, m, :],
                                                     qo[hl_q][r, m, :], start=(hl_k, hl_q) == (1, 0),
                                                     stop=(hl_k, hl_q) == (0, 0))
                                    if (hl_k, hl_q) == (0, 0):
                                        last.then_inc(s2_done, 1)

                        def cross_output(b, m):
                            pe.wait_ge(attn_lo, PAIRS * b + 2 * m + 2)
                            for n in range(2):
                                j = 2 * m + n
                                last = product(pe, bank[OUT_BANK[m]][:, :], at(vb, j), at(attn, j % 4),
                                               n == 0, n == 1)
                            last.then_inc(o_done, 1)

                        def output_rows(b, i):
                            for c in range(EC):
                                if i == 0 and c > 0:
                                    pe.wait_ge(o_lo, EC * b + c + 1)
                                last = product(pe, bank[PROJ_BANK[i]][:, :], at(qo, c, cols(i)), at(wo, c),
                                               c == 0, c == EC - 1)
                            last.then_inc(proj_done, 1)

                        def step(a, b, par):
                            if b is not None:
                                pe.wait_ge(z2T_lo, NB * (b + 1))
                                for m in range(EC):
                                    if m == 1 and not first(b):
                                        pe.wait_ge(x2_ready, NB * b)
                                    project(m, lambda c: at(wq, c, cols(m)), lambda c: at(zT, c), q_done)
                            if a is not None and not first(a):
                                for i in range(NB):
                                    transposed_rows(pe, z1_ready, a, i, 4 + i, z1T_done)
                            if b is not None:
                                pe.wait_ge(kv_ready, len(BLOCKS) * (b + 1))
                                for m in range(2):
                                    pe.wait_ge(q_lo, EC * b + 2 * m + 2)
                                    cross_scores(m)
                            if a is not None:
                                pe.wait_ge(z1T_lo, NB * (a + 1))
                                for m in range(EC):
                                    project(4 + m, lambda c: at(wqk, c, cols(m)), lambda c: at(zT, c), y_done)
                                if b is not None:
                                    pe.wait_ge(s2_masked, PAIRS * b + 4)
                                value_rows(0)
                                pe.wait_ge(y_lo, EC * (a + 1))
                                for i in range(NB):
                                    for c in range(EC):
                                        last = product(pe, bank[0][:, cols(i)], at(yv, c, cols(i)),
                                                       at(zT, c, cols(i)), c == 0, c == EC - 1)
                                last.then_inc(s1_done, 1)
                                value_rows(1)
                            else:
                                for i in range(NB):
                                    transposed_rows(pe, z3_ready, 0, i, FIRST_BANK[i], z3T_done)
                                pe.wait_ge(s2_masked, PAIRS * b + 4)
                            if b is not None:
                                if a is None:
                                    pe.wait_ge(z3T_lo, NB)
                                cross_output(b, 0)
                                cross_output(b, 1)
                                if a is not None:
                                    pe.wait_ge(s1_masked, NB * (a + 1))
                                cross_scores(2)
                                cross_scores(3)
                            if a is not None:
                                pe.wait_ge(prob_ready, NB * (a + 1))
                                pe.wait_ge(v_lo, NB * a + 2)
                                for i in range(NB):
                                    last = pe.transpose(bank[1][:, cols(i)], prob[:, i, :], ident[:, :])
                                last.then_inc(pT_done, 1)
                                if b is not None:
                                    pe.wait_ge(o_lo, EC * b + 2)
                                value_rows(2)
                                value_rows(3)
                                pe.wait_ge(pT_lo, a + 1)
                                if b is not None:
                                    pe.wait_ge(s2_masked, PAIRS * (b + 1))
                                for i in range(NB):
                                    if i >= 2:
                                        pe.wait_ge(v_lo, NB * a + i + 1)
                                    product(pe, bank[BLOCK_BANK[i]][:, :], at(probT, cols(i)), at(yv, i), True, True
                                            ).then_inc(pv_done, 1)
                            if b is not None:
                                cross_output(b, 2)
                                cross_output(b, 3)
                                for i in range(3):
                                    output_rows(b, i)
                            if a is not None:
                                for i in range(NB):
                                    transposed_rows(pe, z2_ready, a, i, BLOCK_BANK[i], z2T_done)
                            if b is not None:
                                output_rows(b, 3)

                        pipeline(pe, step)

        feed = ExitStack()
        with feed:
            sb, pair, sem = names(feed)
            w1p = pair("w1p", [P, EC, FF])
            w2p = pair("w2p", [P, FC, E])
            b1_col = sb("b1_col", [P, FC])
            b2_row = sb("b2_row", [P, E])
            hid = pair("hid", [P, 4, TILE])
            gelu_out = sb("gelu_out", [P, 2, TILE])

            out_stored = [sem(f"out_stored{i}") for i in range(NB)]
            b_loaded, x2_biased = sem("b_loaded"), sem("x2_biased")
            w1_hi, w1_lo, w2_hi, w2_lo = sem("w1_hi"), sem("w1_lo"), sem("w2_hi"), sem("w2_lo")
            up_done, hid_full, hid_lo, out_ready = sem("up_done"), sem("hid_full"), sem("hid_lo"), sem("out_ready")
            down_done, rows_done = sem("down_done"), sem("rows_done")
            DOWNS = FC - 1

            def feed_tiles(engine, step):
                step(0, True, 0)
                with engine.Fori(0, (TILES - 2) // 2) as n:
                    for u in range(2):
                        step(2 * n + u + 1, True, 1 - u)
                step(TILES - 1, False, 1)

            def splits_weights(t):
                return isinstance(t, int) and t == 0

            with nc.Block() as block:
                @block.sync
                def _(sp):
                    def step(t, more, par):
                        if splits_weights(t):
                            sp.dma_start(b1_col[:, :], b1).then_inc(b_loaded, 16)
                            sp.dma_start(b2_row[:, :], b2.partition_broadcast(P)).then_inc(b_loaded, 16)
                            for i in range(NB):
                                sp.wait_ge(x2_stored[i], 16 * TILES)
                                load_x2(sp, 0, 0, i)
                            for c in range(STAGES, FC):
                                sp.wait_ge(w1_lo, c - STAGES + 1)
                                sp.wait_ge(w2_lo, c - STAGES + 1)
                                load_ff_weights(sp, c)
                                if c == 6:
                                    sp.wait_ge(x2_biased, NB)
                                    for i in range(NB):
                                        load_x2(sp, 1, 1, i)
                        elif more:
                            for i in range(NB):
                                sp.wait_ge(out_stored[i], 16 * t)
                                load_x2(sp, t + 1, 1 - par, i)
                        for i in range(NB):
                            sp.wait_ge(out_ready, NB * t + i + 1)
                            sp.dma_start(out_blocks[t * NB + i, :, :], resid[:, par, i, :]
                                         ).then_inc(out_stored[i], 16)

                    feed_tiles(sp, step)
                    for i in range(NB):
                        sp.wait_ge(out_stored[i], 16 * TILES)

                @block.gpsimd
                def _(pool):
                    def add_bias(t, slot):
                        pool.wait_ge(z3_ready, NB * (t + 1))
                        if splits_weights(t):
                            for i in range(NB):
                                pool.wait_ge(x2_loaded[i], 16)
                        for i in range(NB):
                            pool.tensor_tensor(resid[:, slot, i, :], resid[:, slot, i, :], b2_row[:, :], ALU.add
                                               ).then_inc(x2_biased, 1)

                    def split_w2(c):
                        s = c % STAGES
                        pool.wait_ge(w2_loaded[s], 16 * (c // STAGES + 1))
                        pool.tensor_copy(w2p[0][:, c, :], w2_raw[:, s, :]).then_inc(w2_hi, 1)
                        pool.wait_ge(w2_hi, c + 1)
                        pool.tensor_tensor(w2p[1][:, c, :], w2_raw[:, s, :], f(w2p[0][:, c, :]), ALU.subtract
                                           ).then_inc(w2_lo, 1)

                    def step(t, more, par):
                        if splits_weights(t):
                            for c in range(FC):
                                split_w2(c)
                                if c == 3:
                                    add_bias(0, 0)
                        if more:
                            norm_rstd(pool, mv3, ve3, rstd3, ln3, t + 1)
                            add_bias(t + 1, 1 - par)

                    pool.wait_ge(b_loaded, 32)
                    feed_tiles(pool, step)

                @block.scalar
                def _(act):
                    def split_w1(c):
                        act.wait_ge(w1_loaded[c % STAGES], 16 * (c // STAGES + 1))
                        act.activation(w1p[0][:, :, cols(c)], w1_raw[:, c % STAGES, :, :], ACT.Copy
                                       ).then_inc(w1_hi, 1)

                    def step(t, more, par):
                        for c in range(FC):
                            if splits_weights(t) and c + 2 < FC:
                                split_w1(c + 2)
                            act.wait_ge(up_done, FC * t + c + 1)
                            if c >= 4:
                                act.wait_ge(down_done, DOWNS * t + c - 3)
                            act.activation(hid[0][:, c % 4, :], bank[4 + c % 3][:, :], ACT.Gelu,
                                           bias=b1_col[:, c:c + 1])
                            if c >= 2:
                                act.wait_ge(hid_lo, FC * t + c - 1)
                            act.activation(gelu_out[:, c % 2, :], bank[4 + c % 3][:, :], ACT.Gelu,
                                           bias=b1_col[:, c:c + 1]).then_inc(hid_full, 1)
                        if more:
                            for i in range(NB):
                                transpose_high(act, i, LN3_BANK[i], z3T_done, z3T_hi, t + 1)

                    split_w1(0)
                    split_w1(1)
                    act.wait_ge(b_loaded, 32)
                    feed_tiles(act, step)

                @block.vector
                def _(dve):
                    def split_w1(c):
                        dve.wait_ge(w1_hi, c + 1)
                        dve.tensor_tensor(w1p[1][:, :, cols(c)], w1_raw[:, c % STAGES, :, :],
                                          f(w1p[0][:, :, cols(c)]), ALU.subtract).then_inc(w1_lo, 1)

                    def step(t, more, par):
                        for c in range(FC):
                            if splits_weights(t) and c + 2 < FC:
                                split_w1(c + 2)
                            if c == 8 and more:
                                for i in range(NB):
                                    dve.wait_ge(x2_loaded[i], 16 * (t + 2))
                                dve.nop(nofuse=True)
                                norm_stats(dve, lambda i: resid[:, 1 - par, i, :], mv3, ln3, t + 1)
                            if c == 12 and more:
                                dve.wait_ge(z3T_done, NB * (t + 1))
                                norm_rows(dve, lambda i: resid[:, 1 - par, i, :], mv3, rstd3, ln3, t + 1)
                            dve.wait_ge(hid_full, FC * t + c + 1)
                            dve.tensor_tensor(hid[1][:, c % 4, :], gelu_out[:, c % 2, :], f(hid[0][:, c % 4, :]),
                                              ALU.subtract).then_inc(hid_lo, 1)
                        if more:
                            for i in range(NB):
                                transpose_low(dve, i, LN3_BANK[i], z3T_hi, z3T_lo, t + 1)
                        dve.wait_ge(x2_biased, NB * (t + 1))
                        for i in range(NB):
                            dve.wait_ge(rows_done, NB * t + i + 1)
                            dve.tensor_tensor(resid[:, par, i, :], bank[i][:, :], resid[:, par, i, :], ALU.add
                                              ).then_inc(out_ready, 1)

                    split_w1(0)
                    split_w1(1)
                    feed_tiles(dve, step)

                @block.tensor
                def _(pe):
                    def up(t, c):
                        if splits_weights(t):
                            pe.wait_ge(w1_lo, c + 1)
                        if c >= 3:
                            pe.wait_ge(hid_full, FC * t + c - 2)
                        for k in range(EC):
                            last = product(pe, bank[4 + c % 3][:, :], at(w1p, k, cols(c)), at(zT, k),
                                           k == 0, k == EC - 1)
                        last.then_inc(up_done, 1)

                    def down(t, c):
                        if splits_weights(t):
                            pe.wait_ge(w2_lo, c + 1)
                        pe.wait_ge(hid_lo, FC * t + c + 1)
                        if c == 0 and not splits_weights(t):
                            pe.wait_ge(out_ready, NB * t)
                        for i in range(NB):
                            last = product(pe, bank[i][:, :], at(hid, c % 4, cols(i)), at(w2p, c),
                                           c == 0, c == FC - 1)
                            if c == FC - 1:
                                last.then_inc(rows_done, 1)
                        if c < FC - 1:
                            last.then_inc(down_done, 1)

                    def next_rows(t, i):
                        transposed_rows(pe, z3_ready, t + 1, i, LN3_BANK[i], z3T_done)

                    def step(t, more, par):
                        pe.wait_ge(z3T_lo, NB * (t + 1))
                        for c in range(FC):
                            up(t, c)
                            if c >= 2:
                                down(t, c - 2)
                        if more:
                            next_rows(t, 0)
                            pe.wait_ge(hid_full, FC * t + FC - 2)
                            next_rows(t, 1)
                            pe.wait_ge(hid_full, FC * t + FC - 1)
                            next_rows(t, 2)
                        down(t, FC - 2)
                        if more:
                            pe.wait_ge(hid_full, FC * (t + 1))
                            next_rows(t, 3)
                        down(t, FC - 1)

                    feed_tiles(pe, step)


def kernel(x, ctx_1024, mask_Bx1xSxS2_ik1, L0_attn_W_qkv, L0_attn_W_out, L0_attn_b_out, L0_xattn_Wq, L0_xattn_bq,
           L0_xattn_Wk, L0_xattn_bk, L0_xattn_Wv, L0_xattn_bv, L0_xattn_Wo, L0_ffn_w1, L0_ffn_b1, L0_ffn_w2,
           L0_ffn_b2):
    import numpy as np
    import concourse.bacc as bacc
    from concourse.bass_utils import run_bass_kernel_spmd

    def columns(v):
        return np.asarray(v).reshape(-1, P).T

    mask_tiles = np.asarray(mask_Bx1xSxS2_ik1).reshape(TILES, TILE, KEYS).transpose(0, 2, 1)
    laid_out = {
        "x": x, "ctxT": np.asarray(ctx_1024).transpose(2, 0, 1), "mask": mask_tiles,
        "wqkvT": np.asarray(L0_attn_W_qkv).T, "woutT": np.asarray(L0_attn_W_out).T, "b_out": L0_attn_b_out,
        "xwqT": np.asarray(L0_xattn_Wq).T, "bq": columns(L0_xattn_bq),
        "xwkT": np.asarray(L0_xattn_Wk).T, "bk": columns(L0_xattn_bk),
        "xwvT": np.asarray(L0_xattn_Wv).T, "bv": L0_xattn_bv, "xwoT": np.asarray(L0_xattn_Wo).T,
        "w1": L0_ffn_w1, "b1": columns(L0_ffn_b1), "w2": L0_ffn_w2, "b2": L0_ffn_b2,
    }
    nc = bacc.Bacc("TRN2", target_bir_lowering=False, num_devices=1)
    arrays, args = {}, []
    for name, value in laid_out.items():
        a = np.ascontiguousarray(value)
        arrays[f"in_{name}"] = a
        args.append(nc.dram_tensor(f"in_{name}", a.shape, mybir.dt.from_np(a.dtype), kind="ExternalInput").ap())
    args.append(nc.dram_tensor("out_dram", (BATCH, SEQ, E), mybir.dt.float32, kind="ExternalOutput").ap())
    decoder_layer_program(nc, *args)
    result = run_bass_kernel_spmd(nc, [arrays], core_ids=[0])
    return result.results[0]["out_dram"]
```

```python
import concourse.bass as bass
from concourse import mybir
from contextlib import ExitStack

P = 128
BATCH, SEQ, E = 4, 1024, 512
EC = E // P
TILE = 512
NB = TILE // P
TILES = BATCH * SEQ // TILE
TILES_PER_BATCH = SEQ // TILE
KEYS = 64
HEADS, HEAD_DIM = 16, 32
PAIRS = HEADS // 2
HEADS_PER_CHUNK = P // HEAD_DIM
FF = 2048
FC = FF // P
LN_EPS = 1e-5
DEN_EPS = 1e-6
SELF_SCALE = float(E) ** -0.5
CROSS_SCALE = float(HEAD_DIM) ** -0.5
MASKED = -3.0e38
WARM_UP = 9
STAGES = 3

VALUE_BANK = (1, 2, 3, 4)
SELF_BANK = (0, 7)
KEY_BANK = (3, 4)
SCORE_BANK = (0, 1, 2, 3, 5, 6, 7, 0)
OUT_BANK = (3, 4, 5, 1)
BLOCK_BANK = (6, 7, 0, 2)
PROJ_BANK = (3, 4, 5, 1)
LAST_SCORE_BANK = (0, 1, 2, 3, 5, 6, 7, 4)
LAST_OUT_BANK = (0, 1, 5, 6)
LAST_PROJ_BANK = (2, 3, 0, 1)
FIRST_BANK = (4, 5, 6, 7)
LN3_BANK = (7, 5, 6, 4)


def decoder_layer_program(nc, x, ctxT, mask, wqkvT, woutT, b_out, xwqT, bq, xwkT, bk, xwvT, bv, xwoT,
                          w1, b1, w2, b2, out):
    fp32, fp32r, i32 = mybir.dt.float32, mybir.dt.float32r, mybir.dt.int32
    ALU, ACT, AX = mybir.AluOpType, mybir.ActivationFunctionType, mybir.AxisListType

    def product(pe, out_ap, lhs, rhs, start, stop):
        pe.matmul(out_ap, lhs[1], rhs[0], start=start, stop=False)
        pe.matmul(out_ap, lhs[0], rhs[1], start=False, stop=False)
        return pe.matmul(out_ap, lhs[0], rhs[0], start=False, stop=stop)

    def f(ap):
        return ap.bitcast(fp32)

    def cols(n, width=P):
        return slice(n * width, (n + 1) * width)

    x_blocks = x.rearrange("b (n p) e -> (b n) p e", p=P)
    out_blocks = out.rearrange("b (n p) e -> (b n) p e", p=P)
    x2_dram = nc.dram_tensor("x2_dram", (TILES * NB, P, E), fp32).ap()
    keys_dram = nc.dram_tensor("keys_dram", (BATCH, P, EC * KEYS), fp32).ap()
    values_dram = nc.dram_tensor("values_dram", (BATCH, P, E), fp32).ap()

    whole = ExitStack()
    with whole:
        def names(stack):
            def sb(name, shape, dt=fp32):
                return stack.enter_context(nc.sbuf_tensor(name, shape, dt))

            def pair(name, shape):
                return sb(name + "_hi", shape, fp32r), sb(name + "_lo", shape, fp32r)

            def sem(name):
                return stack.enter_context(nc.semaphore(name))
            return sb, pair, sem

        def at(hl, *index):
            return tuple(part[(slice(None),) + index] for part in hl)

        sb, pair, sem = names(whole)
        bank = [whole.enter_context(nc.psum_tensor(f"bank{i}", [P, TILE], fp32)) for i in range(8)]
        ident = sb("ident", [P, P])
        resid = sb("resid", [P, 2, NB, E])
        zn = sb("zn", [P, NB, E])
        zT_parts = sb("zT", [P, 2, EC, TILE], fp32r)
        zT = zT_parts[:, 0, :, :], zT_parts[:, 1, :, :]
        w1_raw = sb("w1_raw", [P, STAGES, EC, P])
        w2_raw = sb("w2_raw", [P, STAGES, E])
        w1_parts = sb("w1_parts", [P, FC, 2, EC, P], fp32r)
        stats, stats1 = sb("stats", [P, NB, 6]), sb("stats1", [P, NB, 6])
        mv1, mv2, mv3 = sb("mv1", [P, NB, 2]), sb("mv2", [P, NB, 2]), sb("mv3", [P, NB, 2])
        ve1, ve2, ve3 = sb("ve1", [P, NB]), sb("ve2", [P, NB]), sb("ve3", [P, NB])
        rstd1, rstd2, rstd3 = sb("rstd1", [P, NB]), sb("rstd2", [P, NB]), sb("rstd3", [P, NB])
        minus_half = sb("minus_half", [P, NB])

        x_loaded = [sem(f"x_loaded{i}") for i in range(NB)]
        x2_stored = [sem(f"x2_stored{i}") for i in range(NB)]
        x2_loaded = [sem(f"x2_loaded{i}") for i in range(NB)]
        w1_loaded = [sem(f"w1_loaded{i}") for i in range(STAGES)]
        w1_hi, w1_lo = sem("w1_hi"), sem("w1_lo")
        w2_loaded = [sem(f"w2_loaded{i}") for i in range(STAGES)]
        ln1, ln2, ln3 = (tuple(sem(f"{n}_{what}") for what in ("stats", "mv", "ve", "rstd", "ready"))
                         for n in ("ln1", "ln2", "ln3"))
        z1_ready, z2_ready, z3_ready = ln1[4], ln2[4], ln3[4]
        z1T_done, z1T_hi, z1T_lo = sem("z1T_done"), sem("z1T_hi"), sem("z1T_lo")
        z2T_done, z2T_hi, z2T_lo = sem("z2T_done"), sem("z2T_hi"), sem("z2T_lo")
        z3T_done, z3T_hi, z3T_lo = sem("z3T_done"), sem("z3T_hi"), sem("z3T_lo")
        filled = sem("filled")

        def chunks(ap):
            return ap.rearrange("p (c t) -> p c t", c=EC)

        def norm_stats(dve, rows_of, mv, ln, t):
            for i in range(NB):
                dve.bn_stats(stats[:, i, :], rows_of(i)).then_inc(ln[0], 1)
            dve.wait_ge(ln[0], NB * t)
            dve.nop(nofuse=True)
            for i in range(NB):
                dve.bn_aggr(mv[:, i, :], stats[:, i, :]).then_inc(ln[1], 1)

        def norm_rstd(pool, mv, ve, rstd, ln, t):
            pool.wait_ge(ln[1], NB * (t + 1))
            pool.nop(nofuse=True)
            pool.tensor_scalar(ve[:, :], mv[:, :, 1], LN_EPS, None, ALU.add).then_inc(ln[2], 1)
            pool.wait_ge(ln[2], t + 1)
            pool.tensor_tensor(rstd[:, :], ve[:, :], minus_half[:, :], ALU.pow).then_inc(ln[3], 1)

        def norm_rows(dve, rows_of, mv, rstd, ln, t):
            dve.wait_ge(ln[3], t + 1)
            for i in range(NB):
                dve.tensor_scalar(zn[:, i, :], rows_of(i), mv[:, i, 0:1], rstd[:, i:i + 1],
                                  ALU.subtract, ALU.mult).then_inc(ln[4], 1)

        def transposed_rows(pe, ready, t, i, to_bank, done):
            pe.wait_ge(ready, NB * t + i + 1)
            for c in range(EC):
                last = pe.transpose(bank[to_bank][:, cols(c)], zn[:, i, cols(c)], ident[:, :])
            last.then_inc(done, 1)

        def transpose_high(act, i, from_bank, done, made, t):
            act.wait_ge(done, NB * t + i + 1)
            act.activation(zT[0][:, :, cols(i)], chunks(bank[from_bank][:, :]), ACT.Copy).then_inc(made, 1)

        def transpose_low(dve, i, from_bank, hi_made, made, t):
            dve.wait_ge(hi_made, NB * t + i + 1)
            dve.tensor_tensor(zT[1][:, :, cols(i)], chunks(bank[from_bank][:, :]), f(zT[0][:, :, cols(i)]),
                              ALU.subtract).then_inc(made, 1)

        def transposed_chunks(pe, t, first_bank):
            pe.wait_ge(z1_ready, NB * (t + 1))
            for c in range(EC):
                for i in range(NB):
                    last = pe.transpose(bank[first_bank + c][:, cols(i)], zn[:, i, cols(c)], ident[:, :])
                last.then_inc(z1T_done, 1)

        def chunk_high(act, t, c, first_bank):
            act.wait_ge(z1T_done, EC * t + c + 1)
            act.activation(zT[0][:, c, :], bank[first_bank + c][:, :], ACT.Copy).then_inc(z1T_hi, 1)

        def chunk_low(dve, t, c, first_bank):
            dve.wait_ge(z1T_hi, EC * t + c + 1)
            dve.tensor_tensor(zT[1][:, c, :], bank[first_bank + c][:, :], f(zT[0][:, c, :]), ALU.subtract
                              ).then_inc(z1T_lo, 1)

        def load_ff_weights(sp, c):
            s = c % STAGES
            sp.dma_start(w1_raw[:, s, :, :], w1[:, cols(c)].rearrange("(c p) n -> p c n", p=P)
                         ).then_inc(w1_loaded[s], 16)
            sp.dma_start(w2_raw[:, s, :], w2[cols(c), :]).then_inc(w2_loaded[s], 16)

        def w1_chunk(c, *k):
            return tuple(w1_parts[(slice(None), c, s) + k] for s in range(2))

        def w1_high(act, c):
            act.wait_ge(w1_loaded[c % STAGES], 16 * (c // STAGES + 1))
            act.activation(w1_chunk(c)[0], w1_raw[:, c % STAGES, :, :], ACT.Copy).then_inc(w1_hi, 1)

        def w1_low(dve, c):
            dve.wait_ge(w1_hi, c + 1)
            dve.tensor_tensor(w1_chunk(c)[1], w1_raw[:, c % STAGES, :, :], f(w1_chunk(c)[0]), ALU.subtract
                              ).then_inc(w1_lo, 1)

        def load_x2(sp, t, slot, i):
            sp.dma_start(resid[:, slot, i, :], x2_dram[t * NB + i, :, :]).then_inc(x2_loaded[i], 16)

        layer = ExitStack()
        with layer:
            sb, pair, sem = names(layer)
            def weight_views(n):
                return tuple(w1_parts[:, 2 * m:2 * m + 2, :, :, :].rearrange("p f s c n -> p (f s c n)")
                             .rearrange("p (c e) -> p c e", c=EC) for m in (2 * n, 2 * n + 1))

            wqk = weight_views(0)
            wvo = weight_views(1)
            wq, wo = weight_views(2), weight_views(3)
            x_in = sb("x_in", [P, NB, E])
            bq_col = sb("bq_col", [P, EC])
            bout_row = sb("bout_row", [P, E])
            causal = sb("causal", [P, P])
            kb_hi, kb_lo = sb("kb_hi", [P, PAIRS, P], fp32r), sb("kb_lo", [P, EC, P], fp32r)
            vb = pair("vb", [P, PAIRS, P])

            bk_col = sb("bk_col", [P, EC])
            qo = pair("qo", [P, EC, TILE])
            attn = pair("attn", [P, 4, TILE])
            ctx2 = tuple(q[:, :, :].rearrange("p c (b d k) -> p c b d k", b=BATCH, d=2) for q in qo)
            wk = attn

            values_stored, wo_lo = sem("values_stored"), sem("wo_lo")
            values = [w2_raw[:, b, :] for b in range(STAGES)]
            values.append(w1_raw[:, 0, :, :].rearrange("p c n -> p (c n)"))

            RAWS = 2 * NB

            def raw(n):
                return resid[:, n % RAWS // NB, n % NB, :]

            def load_x(sp, t, i):
                sp.dma_start(x_in[:, i, :], x_blocks[t * NB + i, :, :]).then_inc(x_loaded[i], 16)

            def next_stats(dve, t, blocks):
                for i in blocks:
                    dve.wait_ge(x_loaded[i], 16 * (t + 1))
                dve.nop(nofuse=True)
                for i in blocks:
                    dve.bn_stats(stats1[:, i, :], x_in[:, i, :]).then_inc(ln1[0], 1)

            setup = ExitStack()
            with setup:
                sb, pair, sem = names(setup)
                PARTS = 8
                part = pair("part", [P, PARTS, E])
                ctx_raw = zn[:, 0:2, :].rearrange("p i (c b k) -> p (i c) b k", c=EC // 2, b=BATCH)
                bv_row = sb("bv_row", [P, E])

                raw_loaded = [sem(f"raw_loaded{i}") for i in range(RAWS)]
                ctx_loaded, bias_loaded = sem("ctx_loaded"), sem("bias_loaded")
                split_hi, split_lo = sem("split_hi"), sem("split_lo")
                ctx_hi, ctx_lo = sem("ctx_hi"), sem("ctx_lo")
                shaped, part_used = sem("shaped"), sem("part_used")
                wqk_done, wvo_done, values_done = sem("wqk_done"), sem("wvo_done"), sem("values_done")
                wqk_hi, wqk_lo, wvo_hi, wvo_lo = sem("wqk_hi"), sem("wqk_lo"), sem("wvo_hi"), sem("wvo_lo")

                CHUNKS = [wqkvT[h * E + c * P:h * E + (c + 1) * P, :] for c in range(EC) for h in (0, 1)]
                for c in range(EC):
                    CHUNKS += [wqkvT[2 * E + c * P:2 * E + (c + 1) * P, :], woutT[cols(c), :]]
                CHUNKS += [w[cols(c), :] for w in (xwvT, xwkT, xwqT, xwoT) for c in range(EC)]
                WO_CHUNK = len(CHUNKS) - EC
                WVO_CHUNK, VALUES_CHUNK = 2 * EC, 4 * EC
                SETUP_ONLY = 5 * EC
                TARGET = [at(part, n % PARTS) for n in range(SETUP_ONLY)]
                TARGET += [at(w, c) for w in (wk, wq, wo) for c in range(EC)]

                with nc.Block() as block:
                    @block.sync
                    def _(sp):
                        for n, w in enumerate(CHUNKS):
                            if n >= RAWS:
                                sp.wait_ge(split_lo, n - RAWS + 1)
                            sp.dma_start(raw(n), w).then_inc(raw_loaded[n % RAWS], 16)
                            if n == RAWS - 1:
                                sp.dma_start(ctx_raw[:, :, :, :], ctxT.rearrange("(c p) b k -> p c b k", p=P)
                                             ).then_inc(ctx_loaded, 16)
                            if n == RAWS + NB - 1:
                                for i in range(NB):
                                    load_x(sp, 0, i)
                                sp.dma_start(bk_col[:, :], bk).then_inc(bias_loaded, 16)
                                sp.dma_start(bq_col[:, :], bq).then_inc(bias_loaded, 16)
                                sp.dma_start(bv_row[:, :], bv.partition_broadcast(P)).then_inc(bias_loaded, 16)
                                sp.dma_start(bout_row[:, :], b_out.partition_broadcast(P)).then_inc(bias_loaded, 16)

                    @block.scalar
                    def _(act):
                        def split_high(n):
                            act.wait_ge(raw_loaded[n % RAWS], 16 * (n // RAWS + 1))
                            if PARTS <= n < SETUP_ONLY:
                                act.wait_ge(part_used, (n - PARTS) // 2 + 1)
                            act.activation(TARGET[n][0], raw(n), ACT.Copy).then_inc(split_hi, 1)

                        def evacuate_high(hl, banks, done, made):
                            act.wait_ge(done, 1)
                            for m in range(EC):
                                act.activation(hl[0][:, m, :], bank[banks + m][:, :], ACT.Copy).then_inc(made, 1)

                        for n in range(8):
                            split_high(n)
                        act.wait_ge(ctx_loaded, 16)
                        for d in range(2):
                            act.activation(ctx2[0][:, :, :, d, :], ctx_raw[:, :, :, :], ACT.Copy
                                           ).then_inc(ctx_hi, 1)
                        for n in range(8, 16):
                            split_high(n)
                        evacuate_high(wqk, 0, wqk_done, wqk_hi)
                        for n in range(16, 24):
                            split_high(n)
                        evacuate_high(wvo, 4, wvo_done, wvo_hi)
                        for c in range(EC):
                            chunk_high(act, 0, c, 0)
                        for n in range(24, 32):
                            split_high(n)

                    @block.vector
                    def _(dve):
                        def split_low(n):
                            dve.wait_ge(split_hi, n + 1)
                            dve.tensor_tensor(TARGET[n][1], raw(n), f(TARGET[n][0]), ALU.subtract
                                              ).then_inc(split_lo, 1)

                        def evacuate_low(hl, banks, hi, made):
                            for m in range(EC):
                                dve.wait_ge(hi, m + 1)
                                dve.tensor_tensor(hl[1][:, m, :], bank[banks + m][:, :], f(hl[0][:, m, :]),
                                                  ALU.subtract).then_inc(made, 1)

                        for n in range(8):
                            split_low(n)
                        for d in range(2):
                            dve.wait_ge(ctx_hi, d + 1)
                            dve.tensor_tensor(ctx2[1][:, :, :, d, :], ctx_raw[:, :, :, :],
                                              f(ctx2[0][:, :, :, d, :]), ALU.subtract).then_inc(ctx_lo, 1)
                        for n in range(8, 12):
                            split_low(n)
                        next_stats(dve, 0, range(NB))
                        dve.wait_ge(ln1[0], NB)
                        for i in range(NB):
                            dve.bn_aggr(mv1[:, i, :], stats1[:, i, :]).then_inc(ln1[1], 1)
                        for n in range(12, 16):
                            split_low(n)
                        norm_rows(dve, lambda i: x_in[:, i, :], mv1, rstd1, ln1, 0)
                        evacuate_low(wqk, 0, wqk_hi, wqk_lo)
                        for n in range(16, 20):
                            split_low(n)
                        evacuate_low(wvo, 4, wvo_hi, wvo_lo)
                        for c in range(EC):
                            chunk_low(dve, 0, c, 0)
                        for n in range(20, WO_CHUNK):
                            split_low(n)
                        dve.wait_ge(bias_loaded, 64)
                        for b in range(BATCH):
                            dve.wait_ge(values_done, b + 1)
                            dve.tensor_tensor(values[b], bank[4 + b][:, :], bv_row[:, :], ALU.add)

                    @block.gpsimd
                    def _(pool):
                        for blocks in (kb_lo, kb_hi, *vb):
                            pool.memset(f(blocks[:, :, :]), 0.0).then_inc(filled, 1)
                        pool.memset(ident[:, :], 0.0).then_inc(filled, 1)
                        pool.memset(causal[:, :], 0.0).then_inc(filled, 1)
                        pool.memset(minus_half[:, :], -0.5).then_inc(filled, 1)
                        pool.wait_ge(filled, 7)
                        pool.affine_select(out=ident[:, :], in_=ident[:, :], compare_op=ALU.not_equal, fill=1.0,
                                           base=0, pattern=[[-1, P]], channel_multiplier=1).then_inc(shaped, 1)
                        pool.affine_select(out=causal[:, :], in_=causal[:, :], compare_op=ALU.is_ge, fill=MASKED,
                                           base=0, pattern=[[-1, P]], channel_multiplier=1).then_inc(shaped, 1)
                        norm_rstd(pool, mv1, ve1, rstd1, ln1, 0)
                        pool.wait_ge(shaped, 2)

                    @block.tensor
                    def _(pe):
                        def fold(first_chunk, banks, done):
                            for c in range(EC):
                                n = first_chunk + 2 * c
                                pe.wait_ge(split_lo, n + 2)
                                for m in range(EC):
                                    last = product(pe, bank[banks + m][:, :], at(part, n % PARTS, cols(m)),
                                                   at(part, (n + 1) % PARTS), c == 0, c == EC - 1)
                                last.then_inc(part_used if c < EC - 1 else done, 1)
                                if c == EC - 1:
                                    pe.wait_ge(done, 1)
                                    pe.sem_inc(part_used, 1)

                        pe.wait_ge(filled, 1)
                        for _ in range(WARM_UP):
                            pe.matmul(bank[7][:, :], kb_lo[:, 0, :], kb_lo[:, :, :].rearrange("p c n -> p (c n)"),
                                      start=True, stop=True)
                        fold(0, 0, wqk_done)
                        fold(WVO_CHUNK, 4, wvo_done)
                        pe.wait_ge(shaped, 2)
                        pe.wait_ge(wqk_lo, EC)
                        transposed_chunks(pe, 0, 0)
                        pe.wait_ge(ctx_lo, 2)
                        for b in range(BATCH):
                            pe.wait_ge(wvo_lo, b + 1)
                            for c in range(EC):
                                if b == 0:
                                    pe.wait_ge(split_lo, VALUES_CHUNK + c + 1)
                                last = product(pe, bank[4 + b][:, :], at(ctx2, c, b),
                                               at(part, (VALUES_CHUNK + c) % PARTS), c == 0, c == EC - 1)
                            last.then_inc(values_done, 1)

            both = ExitStack()
            with both:
                sb, pair, sem = names(both)
                yv = pair("yv", [P, EC, TILE])
                HALVES = cols(0, P // 2), cols(1, P // 2)
                act_in = sb("act_in", [P, 3, TILE])
                keysT = act_in[:, 0:2, :].rearrange("p s (b c k) -> p (s b) c k", b=BATCH // 2, c=EC)
                mask_i = sb("mask_i", [P, TILE], i32)
                mask_f = f(mask_i[:, :])
                keys_now = sb("keys_now", [P, EC, KEYS])
                values_now = sb("values_now", [P, E])
                prob = sb("prob", [P, NB, P])
                probT = pair("probT", [P, TILE])
                nmax, nbias = sb("nmax", [P, NB]), sb("nbias", [P, NB])
                sums, den, rden = sb("sums", [P, NB]), sb("den", [P, NB]), sb("rden", [P, NB])

                mask_loaded, mask_ready = sem("mask_loaded"), sem("mask_ready")
                y_done, s1_done, v_done, pT_done, pv_done = (
                    sem("y_done"), sem("s1_done"), sem("v_done"), sem("pT_done"), sem("pv_done"))
                q_done, s2_done, o_done, proj_done = sem("q_done"), sem("s2_done"), sem("o_done"), sem("proj_done")
                y_hi, v_hi, pT_hi, q_hi, o_hi = sem("y_hi"), sem("v_hi"), sem("pT_hi"), sem("q_hi"), sem("o_hi")
                y_lo, v_lo, pT_lo, q_lo, o_lo = sem("y_lo"), sem("v_lo"), sem("pT_lo"), sem("q_lo"), sem("o_lo")
                s1_large, s1_masked, s1_max, s1_bias, s1_exp, s1_den, s1_rden, prob_ready = (
                    sem("s1_large"), sem("s1_masked"), sem("s1_max"), sem("s1_bias"), sem("s1_exp"), sem("s1_den"),
                    sem("s1_rden"), sem("prob_ready"))
                s2_masked, attn_full, attn_lo = sem("s2_masked"), sem("attn_full"), sem("attn_lo")
                keys_done, keys_out, keys_stored = sem("keys_done"), sem("keys_out"), sem("keys_stored")
                kv_loaded, kv_hi, kv_ready = sem("kv_loaded"), sem("kv_hi"), sem("kv_ready")
                x_biased, x1_ready, x2_ready = sem("x_biased"), sem("x1_ready"), sem("x2_ready")

                BLOCKS, SECOND = [], []
                for h in range(HEADS_PER_CHUNK):
                    r = cols(h, HEAD_DIM)
                    own, other = (kb_hi[cols(at_rows, HEAD_DIM), :, :].rearrange("p (m o) n -> p m o n", o=2)
                                  [:, :, h // 2, cols(h % 2, KEYS)] for at_rows in (h, (h + 2) % HEADS_PER_CHUNK))
                    BLOCKS.append(((own, kb_lo[r, :, cols(h % 2, KEYS)]), keys_now[r, :, :]))
                    SECOND.append((other, keys_now[r, :, :]))
                for h in range(HEADS_PER_CHUNK):
                    r = cols(h % 2, KEYS)
                    BLOCKS.append((
                        tuple(v[r, :, :].rearrange("p (m o) n -> p m o n", o=2)[:, :, h // 2, cols(h, HEAD_DIM)]
                              for v in vb),
                        values_now[r, :].rearrange("p (m h e) -> p m h e", m=EC, e=HEAD_DIM)[:, :, h, :]))

                def self_scores(i, part_):
                    return bank[SELF_BANK[i // 2]][:, :].rearrange(
                        "p (i s n) -> p i s n", i=2, s=2)[:, i % 2, part_, :]

                def key_chunk(m):
                    return bank[KEY_BANK[m // 2]][:, cols(m % 2, BATCH * KEYS)]

                def pipeline(engine, step, last_step, peeled=0):
                    step(0, None, 0)
                    step(1, 0, 1)
                    with engine.Fori(0, (TILES - 2 - peeled) // 2) as n:
                        for u in range(2):
                            step(2 * n + u + 2, 2 * n + u + 1, u)
                    for t in range(TILES - peeled, TILES):
                        step(t, t - 1, t % 2)
                    last_step(TILES - 1)

                def first(t):
                    return isinstance(t, int) and t == 0

                with nc.Block() as block:
                    @block.sync
                    def _(sp):
                        def load_mask(t):
                            for d in range(2):
                                sp.dma_start(mask_i[d * KEYS:(d + 1) * KEYS, :], mask[t, :, :]
                                             ).then_inc(mask_loaded, 16)

                        def load_kv(t):
                            batch = t // TILES_PER_BATCH
                            sp.dma_start(keys_now[:, :, :].rearrange("p c k -> p (c k)"), keys_dram[batch, :, :]
                                         ).then_inc(kv_loaded, 16)
                            sp.dma_start(values_now[:, :], values_dram[batch, :, :]).then_inc(kv_loaded, 16)

                        for b in range(BATCH):
                            sp.dma_start(values_dram[b, :, :], values[b]).then_inc(values_stored, 16)
                        load_mask(0)

                        def step(a, b, par):
                            if b is not None:
                                sp.wait_ge(kv_ready, len(BLOCKS) * (b + 1))
                                load_kv(b + 1)
                                sp.wait_ge(s2_masked, PAIRS * (b + 1))
                                load_mask(b + 1)
                            if isinstance(a, int) and a == TILES - 1:
                                for i in range(NB):
                                    sp.wait_ge(x1_ready, NB * a + i + 1)
                                    sp.dma_start(x_in[:, i, :], x2_dram[i, :, :]).then_inc(x_loaded[i], 16)
                            else:
                                for i in range(NB):
                                    sp.wait_ge(x1_ready, NB * a + i + 1)
                                    load_x(sp, a + 1, i)
                            if b is not None:
                                store_x2(b, 1 - par)
                            else:
                                sp.wait_ge(keys_out, EC)
                                sp.dma_start(keys_dram.rearrange("b p n -> p b n"),
                                             keysT.rearrange("p b c k -> p b (c k)")).then_inc(keys_stored, 16)
                                sp.wait_ge(keys_stored, 16)
                                sp.wait_ge(values_stored, 16 * BATCH)
                                load_kv(0)

                        def store_x2(b, slot):
                            for i in range(NB):
                                sp.wait_ge(x2_ready, NB * b + i + 1)
                                sp.dma_start(x2_dram[b * NB + i, :, :], resid[:, slot, i, :]
                                             ).then_inc(x2_stored[i], 16)

                        def last_step(b):
                            for c in range(STAGES):
                                load_ff_weights(sp, c)

                        pipeline(sp, step, last_step, peeled=2)

                    @block.gpsimd
                    def _(pool):
                        def silu_low(b, j):
                            pool.wait_ge(attn_full, PAIRS * b + j + 1)
                            pool.tensor_tensor(attn[1][:, j % 4, :], act_in[:, j % 3, :], f(attn[0][:, j % 4, :]),
                                               ALU.subtract).then_inc(attn_lo, 1)

                        def step(a, b, par):
                            if b is not None:
                                norm_rstd(pool, mv1, ve1, rstd1, ln1, a)
                                for j in range(4):
                                    silu_low(b, j)
                            pool.wait_ge(z1_ready, NB * (a + 1))
                            for i in range(NB):
                                pool.tensor_tensor(x_in[:, i, :], x_in[:, i, :], bout_row[:, :], ALU.add
                                                   ).then_inc(x_biased, 1)
                            if b is not None:
                                for j in range(4, 8):
                                    silu_low(b, j)
                            else:
                                for c in range(EC):
                                    pool.tensor_tensor(wo[1][:, c, :], raw(WO_CHUNK + c), f(wo[0][:, c, :]),
                                                       ALU.subtract).then_inc(wo_lo, 1)
                            norm_rstd(pool, mv2, ve2, rstd2, ln2, a)

                        def last_step(b):
                            norm_rstd(pool, mv3, ve3, rstd3, ln3, 0)
                            for j in range(PAIRS):
                                silu_low(b, j)

                        pipeline(pool, step, last_step)

                    @block.scalar
                    def _(act):
                        def y_high(a, m):
                            act.wait_ge(y_done, EC * a + m + 1)
                            act.activation(yv[0][:, m, :], bank[4 + m][:, :], ACT.Copy).then_inc(y_hi, 1)

                        def v_high(a, i):
                            act.wait_ge(v_done, NB * a + i + 1)
                            act.activation(yv[0][:, i, :], bank[VALUE_BANK[i]][:, :], ACT.Copy).then_inc(v_hi, 1)

                        def o_high(b, m, banks=OUT_BANK):
                            act.wait_ge(o_done, EC * b + m + 1)
                            act.activation(qo[0][:, m, :], bank[banks[m]][:, :], ACT.Copy).then_inc(o_hi, 1)

                        def silu(b, j):
                            act.wait_ge(s2_masked, PAIRS * b + j + 1)
                            act.activation(attn[0][:, j % 4, :], act_in[:, j % 3, :], ACT.Silu)
                            act.activation(act_in[:, j % 3, :], act_in[:, j % 3, :], ACT.Silu
                                           ).then_inc(attn_full, 1)

                        def keys_high(b):
                            act.wait_ge(kv_loaded, 32 * (b + 1))
                            for hi, source in SECOND + [(hi, source) for (hi, _), source in BLOCKS]:
                                act.activation(hi, source, ACT.Copy).then_inc(kv_hi, 1)

                        def q_high(b, m):
                            act.wait_ge(q_done, EC * b + m + 1)
                            for n, r in enumerate(HALVES):
                                act.activation(qo[n][r, m, :], bank[m][r, :], ACT.Identity,
                                               bias=bq_col[r, m:m + 1]).then_inc(q_hi, 1)

                        def step(a, b, par):
                            if b is not None:
                                keys_high(b)
                                for m in range(EC):
                                    q_high(b, m)
                                for c in range(EC):
                                    chunk_high(act, a, c, 4)
                                for j in range(4):
                                    silu(b, j)
                            for m in range(EC):
                                y_high(a, m)
                            act.wait_ge(s1_bias, a + 1)
                            for i in range(NB):
                                act.activation(prob[:, i, :], prob[:, i, :], ACT.Exp, bias=nbias[:, i:i + 1],
                                               scale=SELF_SCALE, accum_out=sums[:, i:i + 1]
                                               ).then_inc(s1_exp, 1)
                            v_high(a, 0)
                            v_high(a, 1)
                            if b is not None:
                                o_high(b, 0)
                                o_high(b, 1)
                                silu(b, 4)
                                silu(b, 5)
                            else:
                                v_high(a, 2)
                                v_high(a, 3)
                            act.wait_ge(pT_done, a + 1)
                            act.activation(probT[0][:, :], bank[1][:, :], ACT.Copy).then_inc(pT_hi, 1)
                            if b is not None:
                                silu(b, 6)
                                v_high(a, 2)
                                v_high(a, 3)
                                silu(b, 7)
                                o_high(b, 2)
                                o_high(b, 3)
                            else:
                                for m in range(EC):
                                    if m % 2 == 0:
                                        act.wait_ge(keys_done, m // 2 + 1)
                                    act.activation(keysT[:, :, m, :], key_chunk(m).rearrange(
                                        "p (b k) -> p b k", b=BATCH), ACT.Identity, bias=bk_col[:, m:m + 1]
                                        ).then_inc(keys_out, 1)
                            for i in range(NB):
                                transpose_high(act, i, BLOCK_BANK[i], z2T_done, z2T_hi, a)

                        def last_step(b):
                            keys_high(b)
                            for m in range(3):
                                q_high(b, m)
                            silu(b, 0)
                            silu(b, 1)
                            q_high(b, 3)
                            for i in range(NB):
                                transpose_high(act, i, FIRST_BANK[i], z3T_done, z3T_hi, 0)
                            silu(b, 2)
                            o_high(b, 0, LAST_OUT_BANK)
                            silu(b, 3)
                            silu(b, 4)
                            silu(b, 5)
                            o_high(b, 1, LAST_OUT_BANK)
                            silu(b, 6)
                            silu(b, 7)
                            o_high(b, 2, LAST_OUT_BANK)
                            o_high(b, 3, LAST_OUT_BANK)
                            w1_high(act, 0)
                            w1_high(act, 1)

                        pipeline(act, step, last_step)

                    @block.vector
                    def _(dve):
                        def low(hl, m, from_bank, hi_made, made, value):
                            dve.wait_ge(hi_made, value)
                            dve.tensor_tensor(hl[1][:, m, :], bank[from_bank][:, :], f(hl[0][:, m, :]),
                                              ALU.subtract).then_inc(made, 1)

                        def v_low(a, i):
                            low(yv, i, VALUE_BANK[i], v_hi, v_lo, NB * a + i + 1)

                        def o_low(b, m, banks=OUT_BANK):
                            low(qo, m, banks[m], o_hi, o_lo, EC * b + m + 1)

                        def q_low(b, m):
                            for n, r in enumerate(HALVES):
                                dve.wait_ge(q_hi, 2 * (EC * b + m) + n + 1)
                                dve.scalar_tensor_tensor(qo[n][HALVES[1 - n], m, :], bank[m][r, :],
                                                         bq_col[r, m:m + 1], f(qo[n][r, m, :]), ALU.add,
                                                         ALU.subtract).then_inc(q_lo, 1)

                        def mask_scores(b, j, banks=SCORE_BANK):
                            dve.wait_ge(s2_done, PAIRS * b + j + 1)
                            if j >= 3:
                                dve.wait_ge(attn_lo, PAIRS * b + j - 2)
                            dve.scalar_tensor_tensor(act_in[:, j % 3, :], bank[banks[j]][:, :], CROSS_SCALE,
                                                     mask_f[:, :], ALU.mult, ALU.mult).then_inc(s2_masked, 1)

                        def second_residual(b, i, slot, banks=PROJ_BANK):
                            dve.wait_ge(proj_done, NB * b + i + 1)
                            dve.tensor_tensor(resid[:, slot, i, :], bank[banks[i]][:, :], resid[:, slot, i, :],
                                              ALU.add).then_inc(x2_ready, 1)

                        def x1_rows(i, par):
                            return resid[:, par, i, :]

                        def start_step(b, mv, rstd, ln, t):
                            dve.wait_ge(ln1[0], NB * (b + 2))
                            dve.nop(nofuse=True)
                            for i in range(NB):
                                dve.bn_aggr(mv[:, i, :], stats1[:, i, :]).then_inc(ln[1], 1)
                            dve.wait_ge(mask_loaded, 32 * (b + 1))
                            dve.tensor_scalar(mask_f[:, :], mask_i[:, :], 0.0, None, ALU.not_equal
                                              ).then_inc(mask_ready, 1)
                            for rows in (first(b), not first(b)):
                                if rows:
                                    dve.wait_ge(z2T_done, NB * (b + 1))
                                    norm_rows(dve, lambda i: x_in[:, i, :], mv, rstd, ln, t)
                                else:
                                    dve.wait_ge(kv_hi, len(SECOND + BLOCKS) * (b + 1))
                                    for (hi, lo), source in BLOCKS:
                                        dve.tensor_tensor(lo, source, f(hi), ALU.subtract).then_inc(kv_ready, 1)

                        def step(a, b, par):
                            if b is not None:
                                start_step(b, mv1, rstd1, ln1, a)
                                for m in range(EC):
                                    q_low(b, m)
                                for c in range(EC):
                                    chunk_low(dve, a, c, 4)
                                dve.wait_ge(mask_ready, b + 1)
                                for j in range(4):
                                    mask_scores(b, j)
                            for m in range(EC):
                                low(yv, m, 4 + m, y_hi, y_lo, EC * a + m + 1)
                            for i in range(NB):
                                if i % 2 == 0:
                                    dve.wait_ge(s1_done, 2 * a + i // 2 + 1)
                                dve.tensor_tensor(prob[:, i, :], self_scores(i, 0), causal[:, :], ALU.add
                                                  ).then_inc(s1_large, 1)
                            for i in range(NB):
                                dve.wait_ge(s1_large, NB * a + i + 1)
                                dve.tensor_tensor(prob[:, i, :], self_scores(i, 1), prob[:, i, :], ALU.add
                                                  ).then_inc(s1_masked, 1)
                            dve.wait_ge(s1_masked, NB * (a + 1))
                            dve.reduce_max(nmax[:, :], prob[:, :, :], AX.X, negate=True).then_inc(s1_max, 1)
                            dve.wait_ge(s1_max, a + 1)
                            dve.tensor_scalar(nbias[:, :], nmax[:, :], SELF_SCALE, None, ALU.mult
                                              ).then_inc(s1_bias, 1)
                            dve.wait_ge(s1_exp, NB * (a + 1))
                            dve.tensor_scalar(den[:, :], sums[:, :], DEN_EPS, None, ALU.add).then_inc(s1_den, 1)
                            dve.wait_ge(s1_den, a + 1)
                            dve.reciprocal(rden[:, :], den[:, :]).then_inc(s1_rden, 1)
                            dve.wait_ge(s1_rden, a + 1)
                            for i in range(NB):
                                dve.tensor_scalar(prob[:, i, :], prob[:, i, :], rden[:, i:i + 1], None, ALU.mult
                                                  ).then_inc(prob_ready, 1)
                            if b is not None:
                                for i in range(2):
                                    v_low(a, i)
                                    o_low(b, i)
                                for j in range(4, 7):
                                    mask_scores(b, j)
                            else:
                                for i in range(NB):
                                    v_low(a, i)
                            dve.wait_ge(pT_hi, a + 1)
                            dve.tensor_tensor(probT[1][:, :], bank[1][:, :], f(probT[0][:, :]), ALU.subtract
                                              ).then_inc(pT_lo, 1)
                            if b is not None:
                                mask_scores(b, 7)
                                v_low(a, 2)
                                v_low(a, 3)
                            dve.wait_ge(x_biased, NB * (a + 1))
                            for i in range(NB):
                                dve.wait_ge(pv_done, NB * a + i + 1)
                                if b is not None and not first(b):
                                    dve.wait_ge(x2_stored[i], 16 * b)
                                dve.tensor_tensor(x1_rows(i, par), bank[BLOCK_BANK[i]][:, :], x_in[:, i, :],
                                                  ALU.add).then_inc(x1_ready, 1)
                            dve.wait_ge(x1_ready, NB * (a + 1))
                            dve.nop(nofuse=True)
                            for i in range(NB):
                                if b is not None and i in (1, 2):
                                    o_low(b, i + 1)
                                dve.bn_stats(stats[:, i, :], x1_rows(i, par)).then_inc(ln2[0], 1)
                            dve.wait_ge(ln2[0], NB * (a + 1))
                            dve.nop(nofuse=True)
                            for i in range(NB):
                                dve.bn_aggr(mv2[:, i, :], stats[:, i, :]).then_inc(ln2[1], 1)
                            next_stats(dve, a + 1, (0, 1))
                            norm_rows(dve, lambda i: x1_rows(i, par), mv2, rstd2, ln2, a)
                            if b is not None:
                                second_residual(b, 0, 1 - par)
                                second_residual(b, 1, 1 - par)
                                next_stats(dve, a + 1, (2, 3))
                                second_residual(b, 2, 1 - par)
                            for i in range(NB):
                                transpose_low(dve, i, BLOCK_BANK[i], z2T_hi, z2T_lo, a)
                            if b is not None:
                                second_residual(b, 3, 1 - par)
                            else:
                                next_stats(dve, a + 1, (2, 3))

                        def last_step(b):
                            start_step(b, mv3, rstd3, ln3, 0)
                            q_low(b, 0)
                            q_low(b, 1)
                            dve.wait_ge(mask_ready, b + 1)
                            mask_scores(b, 0, LAST_SCORE_BANK)
                            mask_scores(b, 1, LAST_SCORE_BANK)
                            q_low(b, 2)
                            q_low(b, 3)
                            transpose_low(dve, 0, FIRST_BANK[0], z3T_hi, z3T_lo, 0)
                            transpose_low(dve, 1, FIRST_BANK[1], z3T_hi, z3T_lo, 0)
                            mask_scores(b, 2, LAST_SCORE_BANK)
                            transpose_low(dve, 2, FIRST_BANK[2], z3T_hi, z3T_lo, 0)
                            mask_scores(b, 3, LAST_SCORE_BANK)
                            transpose_low(dve, 3, FIRST_BANK[3], z3T_hi, z3T_lo, 0)
                            o_low(b, 0, LAST_OUT_BANK)
                            for j in range(4, PAIRS):
                                mask_scores(b, j, LAST_SCORE_BANK)
                            for m in range(1, EC):
                                o_low(b, m, LAST_OUT_BANK)
                            w1_low(dve, 0)
                            w1_low(dve, 1)
                            for i in range(NB):
                                second_residual(b, i, b % 2, LAST_PROJ_BANK)

                        pipeline(dve, step, last_step)

                    @block.tensor
                    def _(pe):
                        def project(to_bank, lhs, rhs, done):
                            for c in range(EC):
                                last = product(pe, bank[to_bank][:, :], lhs(c), rhs(c), c == 0, c == EC - 1)
                            last.then_inc(done, 1)

                        def value_rows(i):
                            project(VALUE_BANK[i], lambda c: at(zT, c, cols(i)), lambda c: at(wvo, c), v_done)

                        def cross_scores(m, banks=SCORE_BANK):
                            for n, r in enumerate(HALVES):
                                pe.matmul(bank[banks[2 * m + n]][:, :], kb_lo[r, m, :], qo[n][r, m, :],
                                          start=True, stop=False)
                            for n in range(2):
                                pe.matmul(bank[banks[2 * m + n]][:, :], kb_hi[:, 2 * m + n, :], qo[n][:, m, :],
                                          start=False, stop=True).then_inc(s2_done, 1)

                        def cross_output(b, m, banks=OUT_BANK):
                            pe.wait_ge(attn_lo, PAIRS * b + 2 * m + 2)
                            for n in range(2):
                                j = 2 * m + n
                                last = product(pe, bank[banks[m]][:, :], at(vb, j), at(attn, j % 4),
                                               n == 0, n == 1)
                            last.then_inc(o_done, 1)

                        def output_share(i, c, banks=PROJ_BANK):
                            last = product(pe, bank[banks[i]][:, :], at(qo, c, cols(i)), at(wo, c),
                                           c == 0, c == EC - 1)
                            if c == EC - 1:
                                last.then_inc(proj_done, 1)

                        def queries(b, chunks_):
                            pe.wait_ge(z2T_lo, NB * (b + 1))
                            for m in chunks_:
                                if m == 1 and not first(b):
                                    pe.wait_ge(x2_ready, NB * b)
                                project(m, lambda c: at(wq, c, cols(m)), lambda c: at(zT, c), q_done)

                        def step(a, b, par):
                            if b is not None:
                                queries(b, range(EC))
                                transposed_chunks(pe, a, 4)
                                pe.wait_ge(kv_ready, len(BLOCKS) * (b + 1))
                                for m in range(2):
                                    pe.wait_ge(q_lo, 2 * (EC * b + 2 * m + 2))
                                    cross_scores(m)
                            for m, c in [(m, 0) for m in range(EC)] + [(m, c) for m in range(EC)
                                                                       for c in range(1, EC)]:
                                if c == 0:
                                    pe.wait_ge(z1T_lo, EC * a + m + 1)
                                last = product(pe, bank[4 + m][:, :], at(wqk, c, cols(m)), at(zT, c),
                                               c == 0, c == EC - 1)
                                if c == EC - 1:
                                    last.then_inc(y_done, 1)
                            if b is not None:
                                pe.wait_ge(s2_masked, PAIRS * b + 4)
                            value_rows(0)
                            pe.wait_ge(y_lo, EC * (a + 1))
                            for i in range(NB):
                                for c in range(EC):
                                    pe.matmul(self_scores(i, slice(None)), yv[0][:, c, cols(i)],
                                              zT_parts[:, :, c, cols(i)], start=c == 0, stop=False)
                                    last = pe.matmul(self_scores(i, 1), yv[1][:, c, cols(i)],
                                                     zT[0][:, c, cols(i)], start=False, stop=c == EC - 1)
                                if i % 2 == 1:
                                    last.then_inc(s1_done, 1)
                            value_rows(1)
                            if b is not None:
                                cross_output(b, 0)
                                cross_output(b, 1)
                                cross_scores(2)
                                pe.wait_ge(s1_masked, NB * (a + 1))
                                cross_scores(3)
                            else:
                                value_rows(2)
                                value_rows(3)
                            pe.wait_ge(prob_ready, NB * (a + 1))
                            pe.wait_ge(v_lo, NB * a + 1)
                            for i in range(NB):
                                last = pe.transpose(bank[1][:, cols(i)], prob[:, i, :], ident[:, :])
                            last.then_inc(pT_done, 1)
                            if b is not None:
                                for i in (2, 3):
                                    pe.wait_ge(o_lo, EC * b + i - 1)
                                    value_rows(i)
                            pe.wait_ge(pT_lo, a + 1)
                            if b is not None:
                                pe.wait_ge(s2_masked, PAIRS * (b + 1))
                            for i in range(NB):
                                pe.wait_ge(v_lo, NB * a + max(i, 1) + 1)
                                product(pe, bank[BLOCK_BANK[i]][:, :], at(probT, cols(i)), at(yv, i), True, True
                                        ).then_inc(pv_done, 1)
                            if b is not None:
                                cross_output(b, 2)
                                cross_output(b, 3)
                                if first(b):
                                    pe.wait_ge(wo_lo, EC)
                                for i in range(3):
                                    for c in range(EC):
                                        if i == 0:
                                            pe.wait_ge(o_lo, EC * b + c + 1)
                                        output_share(i, c)
                            else:
                                for m in range(EC):
                                    for c in range(EC):
                                        last = product(pe, key_chunk(m), at(wk, c, cols(m)),
                                                       at(ctx2, c, slice(None), 0), c == 0, c == EC - 1)
                                    if m % 2 == 1:
                                        last.then_inc(keys_done, 1)
                            for i in range(NB):
                                transposed_rows(pe, z2_ready, a, i, BLOCK_BANK[i], z2T_done)
                            if b is not None:
                                for c in range(EC):
                                    output_share(3, c)

                        def last_step(b):
                            queries(b, range(3))
                            pe.wait_ge(kv_ready, len(BLOCKS) * (b + 1))
                            pe.wait_ge(q_lo, 2 * (EC * b + 2))
                            cross_scores(0, LAST_SCORE_BANK)
                            queries(b, [3])
                            for i in range(NB):
                                transposed_rows(pe, z3_ready, 0, i, FIRST_BANK[i], z3T_done)
                            pe.wait_ge(q_lo, 2 * (EC * b + 4))
                            cross_scores(1, LAST_SCORE_BANK)
                            cross_output(b, 0, LAST_OUT_BANK)
                            pe.wait_ge(z3T_lo, 3)
                            cross_scores(2, LAST_SCORE_BANK)
                            pe.wait_ge(z3T_lo, 4)
                            cross_scores(3, LAST_SCORE_BANK)
                            pe.wait_ge(s2_masked, PAIRS * b + 4)
                            pe.wait_ge(o_lo, EC * b + 1)
                            output_share(0, 0, LAST_PROJ_BANK)
                            output_share(1, 0, LAST_PROJ_BANK)
                            cross_output(b, 1, LAST_OUT_BANK)
                            output_share(2, 0, LAST_PROJ_BANK)
                            pe.wait_ge(o_lo, EC * b + 2)
                            for i in range(3):
                                output_share(i, 1, LAST_PROJ_BANK)
                            output_share(3, 0, LAST_PROJ_BANK)
                            output_share(3, 1, LAST_PROJ_BANK)
                            cross_output(b, 2, LAST_OUT_BANK)
                            cross_output(b, 3, LAST_OUT_BANK)
                            for c in (2, 3):
                                pe.wait_ge(o_lo, EC * b + c + 1)
                                for i in range(NB):
                                    output_share(i, c, LAST_PROJ_BANK)

                        pipeline(pe, step, last_step)

        feed = ExitStack()
        with feed:
            sb, pair, sem = names(feed)
            w2p = pair("w2p", [P, FC, E])
            b1_col = sb("b1_col", [P, FC])
            b2_row = sb("b2_row", [P, E])
            hid = pair("hid", [P, 4, TILE])
            gelu_out = sb("gelu_out", [P, 2, TILE])

            out_stored = [sem(f"out_stored{i}") for i in range(NB)]
            b_loaded, x2_biased = sem("b_loaded"), sem("x2_biased")
            w2_hi, w2_lo = sem("w2_hi"), sem("w2_lo")
            up_done, hid_full, hid_lo, out_ready = sem("up_done"), sem("hid_full"), sem("hid_lo"), sem("out_ready")
            down_done, rows_done = sem("down_done"), sem("rows_done")
            DOWNS = FC - 1

            def feed_tiles(engine, step):
                step(0, True, 0)
                with engine.Fori(0, (TILES - 2) // 2) as n:
                    for u in range(2):
                        step(2 * n + u + 1, True, 1 - u)
                step(TILES - 1, False, 1)

            def splits_weights(t):
                return isinstance(t, int) and t == 0

            with nc.Block() as block:
                @block.sync
                def _(sp):
                    def step(t, more, par):
                        if splits_weights(t):
                            sp.dma_start(b1_col[:, :], b1).then_inc(b_loaded, 16)
                            sp.dma_start(b2_row[:, :], b2.partition_broadcast(P)).then_inc(b_loaded, 16)
                            for i in range(NB):
                                sp.dma_start(x2_dram[(TILES - 1) * NB + i, :, :], resid[:, (TILES - 1) % 2, i, :]
                                             ).then_inc(x2_stored[i], 16)
                            for i in range(NB):
                                sp.wait_ge(x2_stored[i], 16 * TILES)
                                load_x2(sp, 0, 0, i)
                            for c in range(STAGES, FC):
                                sp.wait_ge(w1_lo, c - STAGES + 1)
                                sp.wait_ge(w2_lo, c - STAGES + 1)
                                load_ff_weights(sp, c)
                                if c == 6:
                                    sp.wait_ge(x2_biased, NB)
                                    for i in range(NB):
                                        load_x2(sp, 1, 1, i)
                        elif more:
                            for i in range(NB):
                                sp.wait_ge(out_stored[i], 16 * t)
                                load_x2(sp, t + 1, 1 - par, i)
                        for i in range(NB):
                            sp.wait_ge(out_ready, NB * t + i + 1)
                            sp.dma_start(out_blocks[t * NB + i, :, :], resid[:, par, i, :]
                                         ).then_inc(out_stored[i], 16)

                    feed_tiles(sp, step)
                    for i in range(NB):
                        sp.wait_ge(out_stored[i], 16 * TILES)

                @block.gpsimd
                def _(pool):
                    def add_bias(t, slot):
                        pool.wait_ge(z3_ready, NB * (t + 1))
                        if splits_weights(t):
                            for i in range(NB):
                                pool.wait_ge(x2_loaded[i], 16)
                        for i in range(NB):
                            pool.tensor_tensor(resid[:, slot, i, :], resid[:, slot, i, :], b2_row[:, :], ALU.add
                                               ).then_inc(x2_biased, 1)

                    def split_w2(c):
                        s = c % STAGES
                        pool.wait_ge(w2_loaded[s], 16 * (c // STAGES + 1))
                        pool.tensor_copy(w2p[0][:, c, :], w2_raw[:, s, :]).then_inc(w2_hi, 1)
                        pool.wait_ge(w2_hi, c + 1)
                        pool.tensor_tensor(w2p[1][:, c, :], w2_raw[:, s, :], f(w2p[0][:, c, :]), ALU.subtract
                                           ).then_inc(w2_lo, 1)

                    def step(t, more, par):
                        if splits_weights(t):
                            for c in range(FC):
                                split_w2(c)
                                if c == 3:
                                    add_bias(0, 0)
                        if more:
                            norm_rstd(pool, mv3, ve3, rstd3, ln3, t + 1)
                            add_bias(t + 1, 1 - par)

                    pool.wait_ge(b_loaded, 32)
                    feed_tiles(pool, step)

                @block.scalar
                def _(act):
                    def step(t, more, par):
                        for c in range(FC):
                            if splits_weights(t) and c + 2 < FC:
                                w1_high(act, c + 2)
                            act.wait_ge(up_done, FC * t + c + 1)
                            if c >= 4:
                                act.wait_ge(down_done, DOWNS * t + c - 3)
                            act.activation(hid[0][:, c % 4, :], bank[4 + c % 3][:, :], ACT.Gelu,
                                           bias=b1_col[:, c:c + 1])
                            if c >= 2:
                                act.wait_ge(hid_lo, FC * t + c - 1)
                            act.activation(gelu_out[:, c % 2, :], bank[4 + c % 3][:, :], ACT.Gelu,
                                           bias=b1_col[:, c:c + 1]).then_inc(hid_full, 1)
                        if more:
                            for i in range(NB):
                                transpose_high(act, i, LN3_BANK[i], z3T_done, z3T_hi, t + 1)

                    act.wait_ge(b_loaded, 32)
                    feed_tiles(act, step)

                @block.vector
                def _(dve):
                    def step(t, more, par):
                        for c in range(FC):
                            if splits_weights(t) and c + 2 < FC:
                                w1_low(dve, c + 2)
                            if c == 8 and more:
                                for i in range(NB):
                                    dve.wait_ge(x2_loaded[i], 16 * (t + 2))
                                dve.nop(nofuse=True)
                                norm_stats(dve, lambda i: resid[:, 1 - par, i, :], mv3, ln3, t + 1)
                            if c == 12 and more:
                                dve.wait_ge(z3T_done, NB * (t + 1))
                                norm_rows(dve, lambda i: resid[:, 1 - par, i, :], mv3, rstd3, ln3, t + 1)
                            dve.wait_ge(hid_full, FC * t + c + 1)
                            dve.tensor_tensor(hid[1][:, c % 4, :], gelu_out[:, c % 2, :], f(hid[0][:, c % 4, :]),
                                              ALU.subtract).then_inc(hid_lo, 1)
                        if more:
                            for i in range(NB):
                                transpose_low(dve, i, LN3_BANK[i], z3T_hi, z3T_lo, t + 1)
                        dve.wait_ge(x2_biased, NB * (t + 1))
                        for i in range(NB):
                            dve.wait_ge(rows_done, NB * t + i + 1)
                            dve.tensor_tensor(resid[:, par, i, :], bank[i][:, :], resid[:, par, i, :], ALU.add
                                              ).then_inc(out_ready, 1)

                    feed_tiles(dve, step)

                @block.tensor
                def _(pe):
                    def up(t, c):
                        if splits_weights(t):
                            pe.wait_ge(w1_lo, c + 1)
                        if c >= 3:
                            pe.wait_ge(hid_full, FC * t + c - 2)
                        for k in range(EC):
                            last = product(pe, bank[4 + c % 3][:, :], w1_chunk(c, k), at(zT, k),
                                           k == 0, k == EC - 1)
                        last.then_inc(up_done, 1)

                    def down(t, c):
                        if splits_weights(t):
                            pe.wait_ge(w2_lo, c + 1)
                        pe.wait_ge(hid_lo, FC * t + c + 1)
                        if c == 0 and not splits_weights(t):
                            pe.wait_ge(out_ready, NB * t)
                        for i in range(NB):
                            last = product(pe, bank[i][:, :], at(hid, c % 4, cols(i)), at(w2p, c),
                                           c == 0, c == FC - 1)
                            if c == FC - 1:
                                last.then_inc(rows_done, 1)
                        if c < FC - 1:
                            last.then_inc(down_done, 1)

                    def next_rows(t, i):
                        transposed_rows(pe, z3_ready, t + 1, i, LN3_BANK[i], z3T_done)

                    def step(t, more, par):
                        pe.wait_ge(z3T_lo, NB * (t + 1))
                        for c in range(FC):
                            up(t, c)
                            if c >= 2:
                                down(t, c - 2)
                        if more:
                            next_rows(t, 0)
                            pe.wait_ge(hid_full, FC * t + FC - 2)
                            next_rows(t, 1)
                            pe.wait_ge(hid_full, FC * t + FC - 1)
                            next_rows(t, 2)
                        down(t, FC - 2)
                        if more:
                            pe.wait_ge(hid_full, FC * (t + 1))
                            next_rows(t, 3)
                        down(t, FC - 1)

                    feed_tiles(pe, step)


def kernel(x, ctx_1024, mask_Bx1xSxS2_ik1, L0_attn_W_qkv, L0_attn_W_out, L0_attn_b_out, L0_xattn_Wq, L0_xattn_bq,
           L0_xattn_Wk, L0_xattn_bk, L0_xattn_Wv, L0_xattn_bv, L0_xattn_Wo, L0_ffn_w1, L0_ffn_b1, L0_ffn_w2,
           L0_ffn_b2):
    import numpy as np
    import concourse.bacc as bacc
    from concourse.bass_utils import run_bass_kernel_spmd

    def columns(v):
        return np.asarray(v).reshape(-1, P).T

    mask_tiles = np.asarray(mask_Bx1xSxS2_ik1).reshape(TILES, TILE, KEYS).transpose(0, 2, 1)
    laid_out = {
        "x": x, "ctxT": np.asarray(ctx_1024).transpose(2, 0, 1), "mask": mask_tiles,
        "wqkvT": np.asarray(L0_attn_W_qkv).T, "woutT": np.asarray(L0_attn_W_out).T, "b_out": L0_attn_b_out,
        "xwqT": np.asarray(L0_xattn_Wq).T, "bq": columns(L0_xattn_bq),
        "xwkT": np.asarray(L0_xattn_Wk).T, "bk": columns(L0_xattn_bk),
        "xwvT": np.asarray(L0_xattn_Wv).T, "bv": L0_xattn_bv, "xwoT": np.asarray(L0_xattn_Wo).T,
        "w1": L0_ffn_w1, "b1": columns(L0_ffn_b1), "w2": L0_ffn_w2, "b2": L0_ffn_b2,
    }
    nc = bacc.Bacc("TRN2", target_bir_lowering=False, num_devices=1)
    arrays, args = {}, []
    for name, value in laid_out.items():
        a = np.ascontiguousarray(value)
        arrays[f"in_{name}"] = a
        args.append(nc.dram_tensor(f"in_{name}", a.shape, mybir.dt.from_np(a.dtype), kind="ExternalInput").ap())
    args.append(nc.dram_tensor("out_dram", (BATCH, SEQ, E), mybir.dt.float32, kind="ExternalOutput").ap())
    decoder_layer_program(nc, *args)
    result = run_bass_kernel_spmd(nc, [arrays], core_ids=[0])
    return result.results[0]["out_dram"]
```
